# Optimizing a Trainium2 kernel written in Bass

```python
import numpy as np
import jax
import jax.numpy as jnp

def _softmax(x, axis=-1):
    return jax.nn.softmax(x, axis=axis)

def _gelu(x):
    return jax.nn.gelu(x, approximate=True)

def _silu(x):
    return jax.nn.silu(x)

def _sigmoid(x):
    return jax.nn.sigmoid(x)

def _layernorm(x, axis=-1, eps=1e-05):
    m = jnp.mean(x, axis=axis, keepdims=True)
    v = jnp.var(x, axis=axis, keepdims=True)
    return (x - m) / jnp.sqrt(v + eps)

def _scatter_add(tgt, idx, src, axis=0):
    return tgt.at[idx].add(src)

def _segment_sum(src, seg, n):
    return jax.ops.segment_sum(src, seg, n)
kernel_name = 'mk_adj_resnorm_d2_adj_r2_215f1f'

def setup_inputs(seed: int=0):
    np.random.seed(seed)
    _w = jnp.asarray

    def _rec_inputs():
        import jax
        import jax.numpy as jnp
        _gk = jax.random.key(seed)
        x = -0.000929 + 1 * jax.random.normal(jax.random.fold_in(_gk, 1), (4096, 128), jnp.float32)
        _w = (1.0 + jnp.arange(4096, dtype=jnp.float32)) ** (-0.5)
        _w = _w / _w.mean()
        _pij = jnp.clip(0.000488281 * _w[:, None] * _w[None, :], 0.0, 1.0)
        _a = jax.random.uniform(jax.random.fold_in(_gk, 2), (4096, 4096)) < _pij
        _a = jnp.logical_or(_a, jnp.eye(4096, dtype=bool))
        _af = _a.astype(jnp.float32)
        adj = _af
        return (x, adj)
    x, adj = _rec_inputs()

    def _L0_gnn_setup():
        import jax, jax.numpy as jnp
        import numpy as np
        N = 4096
        D = 128
        EDGE_P = 0.005
        key = jax.random.key(seed)
        kx, ka, kb = jax.random.split(key, 3)
        x = jax.random.normal(kx, (N, D), dtype=jnp.float32)
        adj = (jax.random.uniform(ka, (N, N)) < EDGE_P).astype(jnp.float32)
        adj = jnp.maximum(adj, jnp.eye(N, dtype=jnp.float32))
        beta = jax.random.uniform(kb, (1,), dtype=jnp.float32)
        return {'x': x, 'adj': adj, 'beta': beta}
    _L0_gnn_all = _L0_gnn_setup()
    _L0_gnn_in = {k: v for k, v in _L0_gnn_all.items() if k in ('beta',)}
    del _L0_gnn_all

    def _L1_gnn_setup():
        import jax, jax.numpy as jnp
        import numpy as np
        N = 5000
        IN_C = 128
        OUT_C = 128
        key = jax.random.key(seed)
        k1, k2, k3 = jax.random.split(key, 3)
        x = jax.random.normal(k1, (N, IN_C), dtype=jnp.float32)
        edge_index = jax.random.uniform(k2, (N, N), dtype=jnp.float32)
        limit = float(np.sqrt(6.0 / (IN_C + OUT_C)))
        weight = jax.random.uniform(k3, (IN_C, OUT_C), dtype=jnp.float32, minval=-limit, maxval=limit)
        return {'x': x, 'edge_index': edge_index, 'weight': weight}
    _L1_gnn_all = _L1_gnn_setup()
    _L1_gnn_in = {k: v for k, v in _L1_gnn_all.items() if k in ('weight',)}
    del _L1_gnn_all
    return {'x': x, 'adj': adj, 'L0_gnn_beta': _L0_gnn_in['beta'], 'L1_gnn_weight': _L1_gnn_in['weight']}

def reference(x, adj, L0_gnn_beta, L1_gnn_weight):
    import jax
    import jax.numpy as jnp

    def _L0_gnn_ref(x, adj, beta):
        import jax, jax.numpy as jnp
        import numpy as np
        N = 4096
        D = 128
        EDGE_P = 0.005
        norm2 = jnp.linalg.norm(x, axis=1, keepdims=True)
        cos = beta[0] * (x @ x.T) / (norm2 @ norm2.T + 1e-07)
        masked = cos + (1.0 - adj) * -1000000000.0
        P = jax.nn.softmax(masked, axis=1)
        return P @ x

    def _L1_gnn_ref(x, edge_index, weight):
        import jax, jax.numpy as jnp
        import numpy as np
        N = 5000
        IN_C = 128
        OUT_C = 128
        support = jnp.matmul(x, weight)
        output = jnp.matmul(edge_index, support)
        return output
    x = _layernorm(x + _L0_gnn_ref(x, adj, L0_gnn_beta), axis=-1)
    x = _layernorm(x + _L1_gnn_ref(x, adj, L1_gnn_weight), axis=-1)
    return x

_drawn_inputs = setup_inputs


def setup_inputs(seed=0):
    import zlib

    import numpy as np

    out = dict(_drawn_inputs(seed))
    spreads = {}
    factors = {}
    for name, (base, spread) in spreads.items():
        noise = np.random.default_rng([zlib.crc32(name.encode()), seed]).standard_normal(out[name].shape)
        drawn = base * np.exp(spread * noise) if base else spread * noise
        out[name] = jnp.asarray(drawn.astype(out[name].dtype))
    for name, factor in factors.items():
        out[name] = (out[name] * factor).astype(out[name].dtype)
    return out
```

```python
from contextlib import ExitStack

import concourse.bass as bass
from concourse import mybir

F32 = mybir.dt.float32
F16 = mybir.dt.float16
BF16 = mybir.dt.bfloat16
U8 = mybir.dt.uint8
I32 = mybir.dt.int32
ALU = mybir.AluOpType
ACT = mybir.ActivationFunctionType
AX = mybir.AxisListType
RMAX = bass.bass_isa.ReduceOp.max
RADD = bass.bass_isa.ReduceOp.add

P = 128
EPS_LN = 1e-5
EPS_COS = 1e-7


def resnorm_graph_kernel(nc, x, adj, beta, weight, x1_dram, sup_dram, q_dram, out):
    N, D = x.shape
    BI = 512
    NB = N // BI
    IT = BI // P
    NT = N // P
    UT = 4
    NU = NT // UT
    WT = 2 * UT
    NW = NT // WT
    XC = 2 * D + 1
    ESC = 2.0 ** 15
    USC = 2.0 ** 15
    assert D == P and NB % 2 == 0 and NW > 1

    with ExitStack() as ctx:
        def sb(name, shape, dt):
            return ctx.enter_context(nc.sbuf_tensor(name, shape, dt))

        def sem(name):
            return ctx.enter_context(nc.semaphore(name))

        adjT = sb("adjT", [P, NB, NT, BI], U8)
        stage = sb("stage", [P, 2, IT, UT * P], F32)
        uT = sb("uT", [P, 2, N], F16)
        xaug = sb("xaug", [P, NT, XC], F16)
        E = sb("E", [P, UT, BI], F32)
        eh = sb("eh", [P, UT, BI], F16)
        el = sb("el", [P, UT, BI], F16)
        xres = sb("xres", [P, IT, D], F32)
        h = sb("h", [P, IT, D], F32)
        x1 = sb("x1", [P, IT, D], F32)
        sup32 = sb("sup32", [P, IT, D], F32)
        x1T = sup32[:, :, :].rearrange("p t d -> p (t d)")
        q_row = sb("q_row", [P, BI], F32)
        q_T = sb("q_T", [NT, P], F32)
        flag = sb("flag", [P, 1], I32)
        sup2 = sb("sup2", [P, IT, 2, D], F16)
        w_sb = sb("w_sb", [P, D], F32)
        ident = sb("ident", [P, P], F32)
        identb = sb("identb", [P, P], BF16)
        zeros = sb("zeros", [P, P], F16)
        n2 = sb("n2", [P, NT], F32)
        rn = sb("rn", [P, NT], F32)
        q = sb("q", [P, NT], F32)
        rnu = sb("rnu", [P, NT], F32)
        half_pow = sb("half_pow", [P, NT], F32)
        sc = sb("sc", [P, 17], F32)
        stats = sb("stats", [P, 8, 6], F32)
        mean = sb("mean", [P, 8], F32)
        tmp = sb("tmp", [P, 3, 8], F32)
        rstd = sb("rstd", [P, 8], F32)
        rden = sb("rden", [P, IT], F32)

        xfull = adjT[:, NB - 1, :, :].rearrange("p t i -> p (t i)").bitcast(F32).rearrange("p (t d) -> p t d", d=D)
        work = adjT[:, NB - 2, :, :].rearrange("p t i -> p (t i)").bitcast(F32).rearrange("p (t d) -> p t d", d=D)
        xsc = adjT[:, NB - 3, :, :].rearrange("p t i -> p (t i)").bitcast(F32).rearrange("p (t d) -> p t d", d=D)
        sup_all = uT[:, :, :].rearrange("p a (t d) -> p (a t) d", d=2 * D)
        adjb = E[:, :, :].rearrange("p a i -> p (a i)").bitcast(BF16).rearrange("p (s i) -> p s i", i=2 * BI)

        C_RMAX, C_QMAX, C_FRO, C_G0, C_G1, C_G2 = 0, 1, 2, 3, 4, 5
        C_PX, C_PF, C_XS, C_XI, C_SS, C_SI, C_B, C_BS, C_BB, C_T, C_T2 = range(6, 17)

        def col(c):
            return sc[:, c:c + 1]

        psum = ctx.enter_context(nc.psum_tensor("psum", [P, 8, 512], F32))
        S = [psum[:, b, :] for b in range(2)]
        T = [psum[:, 2 + b, :].bitcast(BF16).rearrange("p (t i) -> p t i", i=BI) for b in range(2)]
        O = [psum[:, 4 + b, :] for b in range(IT)]

        CB = [4, 0]

        x_in = sem("x_in")
        w_in = sem("w_in")
        beta_in = sem("beta_in")
        adj_in = [sem(f"adj_in{b}") for b in range(2)]
        xres_in = sem("xres_in")
        consts = sem("consts")
        q_filled = sem("q_filled")
        q_moved = sem("q_moved")
        q_stored = sem("q_stored")
        q_row_in = sem("q_row_in")
        flag_set = sem("flag_set")
        half_scaled = sem("half_scaled")
        scaled = sem("scaled")
        fix = sem("fix")
        pro = sem("pro")
        gp = sem("gp")
        uT_filled = sem("uT_filled")
        uT_hi = sem("uT_hi")
        uT_lo = sem("uT_lo")
        slot_filled = sem("slot_filled")
        slot_done = sem("slot_done")
        mask_filled = sem("mask_filled")
        mask_stored = sem("mask_stored")
        masked = sem("masked")
        hi_done = sem("hi_done")
        lo_done = sem("lo_done")
        pv_done = sem("pv_done")
        o_read = sem("o_read")
        chain = sem("chain")
        stats_done = sem("stats_done")
        rstd_done = sem("rstd_done")
        x1_done = sem("x1_done")
        x1_stored = sem("x1_stored")
        sup_hi = sem("sup_hi")
        sup_split = sem("sup_split")
        u_done = sem("u_done")
        sup_stored = sem("sup_stored")
        sup_in = sem("sup_in")
        adjb_v = sem("adjb_v")
        adjb_a = sem("adjb_a")
        agg_done = sem("agg_done")
        c_ready = sem("c_ready")
        c_read = sem("c_read")
        x1_in = [sem(f"x1_in{b}") for b in range(2)]
        y_done = sem("y_done")
        y_stored = sem("y_stored")

        adj_v = adj.rearrange("(b t p) (u c) -> b u p t c", p=P, t=IT, c=UT * P)
        x_v = x.rearrange("(b t p) d -> b p t d", p=P, t=IT)
        x1_v = x1_dram.rearrange("(b t p) d -> b p t d", p=P, t=IT)
        sup_v = sup_dram.rearrange("(b t p) d -> b p t d", p=P, t=IT)
        sup_l = sup_dram.rearrange("(t p) d -> p t d", p=P)
        q_v = q_dram.rearrange("a (t p) -> (a t) p", p=P)
        out_v = out.rearrange("(b t p) d -> b p t d", p=P, t=IT)

        block = ctx.enter_context(nc.Block())

        def slots_before(b):
            return b * (NT + 2) - 2

        def slot_of(b, w, k):
            if isinstance(b, int) and b == 0:
                return w * WT + k
            if isinstance(w, int) and w == 0:
                return slots_before(b) + k + (1 if k >= UT + 2 else 0)
            return slots_before(b) + 2 + w * WT + k

        def bank_of(b, w, k):
            late = not (isinstance(b, int) and b == 0) and isinstance(w, int) and w == 0 and k >= UT + 2
            return (k + late) % 2

        def first(b, w):
            return isinstance(b, int) and b == 0 and isinstance(w, int) and w == 0

        @block.sync
        def _(sp):
            for c in range(4):
                s = slice(c * NT // 4, (c + 1) * NT // 4)
                sp.dma_start(xfull[:, s, :], x.rearrange("(t p) d -> p t d", p=P)[:, s, :]).then_inc(x_in, 16)
            sp.dma_start(w_sb[:, :], weight).then_inc(w_in, 16)
            sp.dma_start(col(C_B), beta.rearrange("(a b) -> a b", a=1).to_broadcast([P, 1])).then_inc(beta_in, 16)

            def load_unit(b, u, slot):
                sp.dma_start(stage[:, slot, :, :], adj_v[b, u, :, :, :]).then_inc(adj_in[slot], 16)

            def load_units(b, w):
                for s in range(2):
                    if not first(b, w):
                        sp.wait_ge(mask_filled, (b * NU + 2 * w + s - 1) * 2)
                    load_unit(b, 2 * w + s, s)

            def store_block(b):
                sp.wait_ge(x1_done, b + 1)
                sp.dma_start(x1_v[b], x1[:, :, :]).then_inc(x1_stored, 16)
                sp.wait_ge(sup_split, b + 1)
                sp.dma_start(sup_v[b], sup2[:, :, :, :].rearrange("p t a d -> p t (a d)")).then_inc(sup_stored, 16)

            def load_xres(b):
                sp.dma_start(xres[:, :, :], x_v[b]).then_inc(xres_in, 16)

            def load_q_row(b):
                if not isinstance(b, int) or b > 0:
                    sp.wait_ge(masked, NT * b)
                sp.dma_start(q_row[:, :], q_dram[0:1, bass.ds(b * BI, BI)].to_broadcast([P, BI])).then_inc(q_row_in, 16)

            load_xres(0)
            load_units(0, 0)
            sp.wait_ge(q_moved, 1)
            sp.dma_start(q_v, q_T[:, :]).then_inc(q_stored, 16)
            sp.wait_ge(q_stored, 16)
            load_q_row(0)
            with sp.Fori(1, NW) as w:
                load_units(0, w)
            with sp.Fori(1, NB) as b:
                load_units(b, 0)
                load_q_row(b)
                load_units(b, 1)
                store_block(b - 1)
                load_xres(b)
                with sp.Fori(2, NW) as w:
                    load_units(b, w)
            store_block(NB - 1)
            sp.wait_ge(slot_filled, slots_before(NB))
            sp.wait_ge(sup_stored, 16 * NB)
            sp.dma_start(sup_all, sup_l).then_inc(sup_in, 16)
            sp.wait_ge(x1_stored, 16 * NB)
            for r in range(NB):
                if r >= 2:
                    sp.wait_ge(y_stored, 16 * (r - 1))
                sp.dma_start(stage[:, r % 2, :, 0:D], x1_v[r]).then_inc(x1_in[r % 2], 16)
                if r >= 1:
                    sp.wait_ge(y_done, r)
                    sp.dma_start(out_v[r - 1], stage[:, (r - 1) % 2, :, 2 * D:3 * D]).then_inc(y_stored, 16)
            sp.wait_ge(y_done, NB)
            sp.dma_start(out_v[NB - 1], stage[:, (NB - 1) % 2, :, 2 * D:3 * D]).then_inc(y_stored, 16)
            sp.wait_ge(y_stored, 16 * NB)

        @block.gpsimd
        def _(pool):
            nc.gpsimd.memset(ident[:, :], 0.0).then_inc(consts, 1)
            nc.gpsimd.memset(zeros[:, :], 0.0).then_inc(consts, 1)
            nc.gpsimd.memset(xaug[:, :, D:D + 1], 1.0).then_inc(consts, 1)
            nc.gpsimd.memset(half_pow[:, :], -0.5).then_inc(consts, 1)
            pool.wait_ge(consts, 4)
            nc.gpsimd.affine_select(out=ident[:, :], in_=ident[:, :], compare_op=ALU.not_equal, fill=1.0,
                                    base=0, pattern=[[-1, P]], channel_multiplier=1).then_inc(consts, 1)
            pool.wait_ge(consts, 5)
            nc.gpsimd.tensor_copy(identb[:, :], ident[:, :]).then_inc(consts, 1)
            pool.wait_ge(pro, 3)
            nc.gpsimd.tensor_tensor(rn[:, :], n2[:, :], half_pow[:, :], ALU.pow).then_inc(gp, 1)
            pool.wait_ge(pro, 7)
            nc.gpsimd.partition_all_reduce(sc[:, C_G0:C_G0 + 2], sc[:, C_RMAX:C_RMAX + 2], P, RMAX).then_inc(gp, 1)
            nc.gpsimd.partition_all_reduce(col(C_G2), col(C_FRO), P, RADD).then_inc(gp, 1)

            def rsqrt_rows(done, c):
                pool.wait_ge(stats_done, done)
                nc.gpsimd.tensor_tensor(rstd[:, c:c + IT], rstd[:, c:c + IT], half_pow[:, 0:IT],
                                        ALU.pow).then_inc(rstd_done, 1)

            with pool.Fori(1, NB + 1) as b:
                rsqrt_rows(b, 0)
            for r in range(NB):
                rsqrt_rows(NB + r + 1, IT * (r % 2))

        @block.scalar
        def _(act):
            for g in range(NT // 4):
                act.wait_ge(uT_filled, g + 1)
                nc.scalar.activation(uT[:, 0, g * 512:(g + 1) * 512], psum[:, g % 4, :], ACT.Copy).then_inc(uT_hi, 1)
            act.wait_ge(q_filled, 1)
            nc.scalar.activation(q_T[:, :], psum[0:NT, 4, 0:P], ACT.Copy).then_inc(q_moved, 1)
            act.wait_ge(pro, 10)
            act.wait_ge(flag_set, 1)
            small = act.value_load(flag[0:1, 0:1], min_val=0, max_val=1)

            def exp_tile(b, w, k):
                c = slot_of(b, w, k)
                n = b * NT + w * WT + k
                act.wait_ge(slot_filled, c + 1)
                act.wait_ge(scaled, (n + 1) * small + 1)
                if not (first(b, w) and k < UT):
                    act.wait_ge(lo_done, n - UT + 1)
                nc.scalar.activation(E[:, k % UT, :], S[bank_of(b, w, k)], ACT.Exp,
                                     bias=col(C_BB), scale=col(C_BS)).then_inc(slot_done, 1)

            def store_masks(b, w, k):
                p = (b * NT + w * WT + k) // 2 if isinstance(b, int) and isinstance(w, int) else b * (NT // 2) + w * UT + k // 2
                act.wait_ge(mask_filled, p + 1)
                nc.scalar.activation(adjT[:, b, bass.ds(w * WT + k, 2), :], T[(k // 2) % 2], ACT.Copy).then_inc(mask_stored, 1)

            def rows_T(b, slot):
                act.wait_ge(slot_filled, slot + 1)
                if not isinstance(b, int) or b > 0:
                    act.wait_ge(sup_split, b)
                nc.scalar.activation(x1T, S[0], ACT.Copy).then_inc(slot_done, 1)

            def sup_out(b, slot):
                act.wait_ge(slot_filled, slot + 1)
                nc.scalar.activation(sup32[:, :, :].rearrange("p t d -> p (t d)"), S[1], ACT.Copy,
                                     scale=col(C_SS)).then_inc(slot_done, 1)

            def step(b, w):
                for k in range(0, WT, 2):
                    store_masks(b, w, k)
                    exp_tile(b, w, k)
                    exp_tile(b, w, k + 1)

            step(0, 0)
            with act.Fori(1, NW) as w:
                step(0, w)
            with act.Fori(1, NB) as b:
                for k in range(0, UT + 2, 2):
                    store_masks(b, 0, k)
                    exp_tile(b, 0, k)
                    exp_tile(b, 0, k + 1)
                rows_T(b - 1, slots_before(b) + UT + 2)
                store_masks(b, 0, UT + 2)
                exp_tile(b, 0, UT + 2)
                exp_tile(b, 0, UT + 3)
                sup_out(b - 1, slots_before(b) + WT + 1)
                with act.Fori(1, NW) as w:
                    step(b, w)
            rows_T(NB - 1, slots_before(NB))
            sup_out(NB - 1, slots_before(NB) + 1)

            def widen(r, g):
                for s in (1, 3):
                    if not (r == 0 and isinstance(g, int)):
                        act.wait_ge(agg_done, r * NT + g * 4 + s - 3)
                    nc.scalar.activation(adjb[:, s, :].rearrange("p (b i) -> p b i", i=BI),
                                         adjT[:, 2 * r:2 * r + 2, g * 4 + s, :], ACT.Copy).then_inc(adjb_a, 1)

            act.wait_ge(lo_done, NB * NT)
            widen(0, 0)
            for r in range(NB // 2):
                with act.Fori(int(r == 0), NT // 4) as g:
                    widen(r, g)

        @block.vector
        def _(dve):
            dve.wait_ge(x_in, 64)
            nc.vector.tensor_tensor(work, xfull, xfull, ALU.mult).then_inc(pro, 1)
            dve.wait_ge(pro, 1)
            nc.vector.tensor_reduce(n2[:, :], work, op=ALU.add, axis=AX.X).then_inc(pro, 1)
            dve.wait_ge(pro, 2)
            nc.vector.tensor_scalar_max(n2[:, :], n2[:, :], 1e-36).then_inc(pro, 1)
            dve.wait_ge(gp, 1)
            nc.vector.reciprocal(q[:, :], rn[:, :]).then_inc(pro, 1)
            nc.vector.reduce_max(col(C_RMAX), rn[:, :], AX.X).then_inc(pro, 1)
            dve.wait_ge(pro, 4)
            nc.vector.reduce_max(col(C_QMAX), q[:, :], AX.X).then_inc(pro, 1)
            dve.wait_ge(w_in, 16)
            nc.vector.tensor_tensor_reduce(out=x1[:, 0, :], in0=w_sb[:, :], in1=w_sb[:, :], scale=1.0, scalar=0.0,
                                           op0=ALU.mult, op1=ALU.add, accum_out=col(C_FRO)).then_inc(pro, 1)
            nc.vector.tensor_scalar_mul(rnu[:, :], rn[:, :], USC).then_inc(pro, 1)
            dve.wait_ge(pro, 8)
            for t in range(NT):
                last = nc.vector.tensor_scalar_mul(work[:, t, :], xfull[:, t, :], rnu[:, t:t + 1])
                if t % 4 == 3:
                    last.then_inc(u_done, 1)
            dve.wait_ge(beta_in, 16)
            nc.vector.tensor_scalar_mul(col(C_BS), col(C_B), 1.0 / (USC * USC)).then_inc(pro, 1)
            nc.vector.tensor_scalar(col(C_BB), col(C_B), -1.0, col(C_B), ALU.mult, ALU.min).then_inc(pro, 1)
            dve.wait_ge(gp, 3)
            nc.vector.tensor_scalar(sc[:, C_PX:C_PX + 1].bitcast(I32), col(C_G1).bitcast(I32), 0x7F800000, None,
                                    ALU.bitwise_and).then_inc(pro, 1)
            nc.vector.tensor_scalar(sc[:, C_PF:C_PF + 1].bitcast(I32), col(C_G2).bitcast(I32), 0x7F800000, None,
                                    ALU.bitwise_and).then_inc(pro, 1)
            dve.wait_ge(pro, 12)
            nc.vector.reciprocal(col(C_XS), col(C_PX)).then_inc(pro, 1)
            nc.vector.tensor_scalar_mul(col(C_XI), col(C_PX), 2.0 ** -14).then_inc(pro, 1)
            dve.wait_ge(pro, 14)
            nc.vector.tensor_scalar(xsc, xfull, col(C_XS), 2.0 ** 14, ALU.mult, ALU.mult).then_inc(pro, 1)
            dve.wait_ge(pro, 15)
            nc.vector.tensor_copy(xaug[:, :, 0:D], xsc).then_inc(pro, 1)
            dve.wait_ge(pro, 16)
            nc.vector.tensor_tensor(xaug[:, :, D + 1:XC], xsc, xaug[:, :, 0:D], ALU.subtract).then_inc(pro, 1)
            nc.vector.tensor_scalar_max(col(C_T), col(C_PF), 1e-30).then_inc(pro, 1)
            dve.wait_ge(pro, 18)
            nc.vector.reciprocal(col(C_SS), col(C_T)).then_inc(pro, 1)
            nc.vector.tensor_scalar_mul(col(C_SI), col(C_T), 1.0).then_inc(pro, 1)
            dve.wait_ge(gp, 3)
            nc.vector.tensor_tensor(col(C_T2), col(C_G0), col(C_G0), ALU.mult).then_inc(fix, 1)
            dve.wait_ge(fix, 1)
            nc.vector.tensor_scalar(flag[:, :], col(C_T2), 0.5, None, ALU.is_gt).then_inc(flag_set, 1)
            dve.wait_ge(flag_set, 1)
            nc.vector.tensor_copy(col(C_T2), flag[:, :]).then_inc(scaled, 1)
            small = dve.value_load(flag[0:1, 0:1], min_val=0, max_val=1)
            for g in range(NT // 4):
                dve.wait_ge(uT_hi, g + 1)
                nc.vector.tensor_tensor(uT[:, 1, g * 512:(g + 1) * 512], psum[:, g % 4, :],
                                        uT[:, 0, g * 512:(g + 1) * 512], ALU.subtract).then_inc(uT_lo, 1)

            HB = BI // 2

            def add_small_term(b, w, k):
                n = b * NT + w * WT + k
                dve.wait_ge(slot_filled, slot_of(b, w, k) + 1)
                dve.wait_ge(q_row_in, 16 * (b + 1))
                if not (first(b, w) and k < UT):
                    dve.wait_ge(lo_done, n - UT + 1)
                num, den = E[:, k % UT, 0:HB], E[:, k % UT, HB:BI]
                s = S[bank_of(b, w, k)]
                for half in range(2):
                    base = 1 + 8 * n + 4 * half
                    part = slice(half * HB, (half + 1) * HB)
                    nc.vector.tensor_scalar_mul(num, q_row[:, part], q[:, bass.ds(w * WT + k, 1)]).then_inc(fix, 1)
                    dve.wait_ge(fix, base + 1)
                    nc.vector.tensor_scalar_add(den, num, EPS_COS).then_inc(fix, 1)
                    dve.wait_ge(fix, base + 2)
                    nc.vector.reciprocal(den, den).then_inc(fix, 1)
                    dve.wait_ge(fix, base + 3)
                    nc.vector.tensor_tensor(num, num, den, ALU.mult).then_inc(fix, 1)
                    dve.wait_ge(fix, base + 4)
                    done = nc.vector.tensor_tensor(s[:, part], s[:, part], num, ALU.mult)
                    done.then_inc(half_scaled, 1) if half == 0 else done.then_inc(scaled, 1)
                    if half == 0:
                        dve.wait_ge(half_scaled, n + 1)

            def mask_tile(b, w, k):
                n = b * NT + w * WT + k
                with dve.If(small > 0):
                    add_small_term(b, w, k)
                p = b * (NT // 2) + w * UT + k // 2
                dve.wait_ge(slot_done, slot_of(b, w, k) + 1)
                dve.wait_ge(mask_stored, p + 1)
                nc.vector.scalar_tensor_tensor(out=E[:, k % UT, :], in0=E[:, k % UT, :], scalar=ESC,
                                               in1=adjT[:, b, w * WT + k, :], op0=ALU.mult,
                                               op1=ALU.mult).then_inc(masked, 1)

            def split_hi(n, k, fresh=False):
                dve.wait_ge(masked, n + 1)
                if not fresh:
                    dve.wait_ge(pv_done, n - UT + 1)
                nc.vector.tensor_copy(eh[:, k % UT, :], E[:, k % UT, :]).then_inc(hi_done, 1)

            def split_lo(n, k):
                dve.wait_ge(hi_done, n + 1)
                nc.vector.tensor_tensor(el[:, k % UT, :], E[:, k % UT, :], eh[:, k % UT, :],
                                        ALU.subtract).then_inc(lo_done, 1)

            def step(b, w, ks=range(WT)):
                for k in ks:
                    n = b * NT + w * WT + k
                    mask_tile(b, w, k)
                    if not (first(b, w) and k == 0):
                        split_lo(n - 1, k - 1)
                    split_hi(n, k, first(b, w) and k < UT)

            def layer_stats(src, o, base):
                for t in range(IT):
                    last = nc.vector.bn_stats(stats[:, o + t, :], src(t))
                last.then_inc(chain, 1)
                dve.wait_ge(chain, base + 1)
                s_ = slice(o, o + IT)
                nc.vector.tensor_tensor(tmp[:, 0, s_], stats[:, s_, 1], stats[:, s_, 4], ALU.add)
                nc.vector.tensor_tensor(tmp[:, 1, s_], stats[:, s_, 1], stats[:, s_, 4], ALU.subtract)
                nc.vector.tensor_tensor(tmp[:, 2, s_], stats[:, s_, 2], stats[:, s_, 5], ALU.add).then_inc(chain, 1)
                dve.wait_ge(chain, base + 2)
                nc.vector.tensor_scalar(tmp[:, 2, s_], tmp[:, 2, s_], 1.0 / D, EPS_LN, ALU.mult, ALU.add)
                nc.vector.scalar_tensor_tensor(out=tmp[:, 1, s_], in0=tmp[:, 1, s_], scalar=0.25, in1=tmp[:, 1, s_],
                                               op0=ALU.mult, op1=ALU.mult)
                nc.vector.tensor_scalar_mul(mean[:, s_], tmp[:, 0, s_], 0.5).then_inc(chain, 1)
                dve.wait_ge(chain, base + 3)
                nc.vector.tensor_tensor(rstd[:, s_], tmp[:, 1, s_], tmp[:, 2, s_], ALU.add).then_inc(stats_done, 1)

            def normalise(dst, src, o, done):
                dve.wait_ge(rstd_done, done)
                for t in range(IT):
                    last = nc.vector.tensor_scalar(dst(t), src(t), mean[:, o + t:o + t + 1],
                                                   rstd[:, o + t:o + t + 1], ALU.subtract, ALU.mult)
                return last

            def norm_rows(b):
                if not isinstance(b, int) or b > 0:
                    dve.wait_ge(x1_stored, 16 * b)
                normalise(lambda t: x1[:, t, :], lambda t: h[:, t, :], 0, b + 1).then_inc(x1_done, 1)

            def split_sup(b, slot):
                dve.wait_ge(slot_done, slot + 1)
                if not isinstance(b, int) or b > 0:
                    dve.wait_ge(sup_stored, 16 * b)
                nc.vector.tensor_copy(sup2[:, :, 0, :], sup32[:, :, :]).then_inc(sup_hi, 1)
                dve.wait_ge(sup_hi, b + 1)
                nc.vector.tensor_tensor(sup2[:, :, 1, :], sup32[:, :, :], sup2[:, :, 0, :],
                                        ALU.subtract).then_inc(sup_split, 1)

            def rows(b):
                dve.wait_ge(pv_done, (b + 1) * NT)
                dve.wait_ge(xres_in, 16 * (b + 1))
                nc.vector.reciprocal(rden[:, :], psum[:, 4:4 + IT, D]).then_inc(chain, 1)
                dve.wait_ge(chain, 6 * b + 1)
                nc.vector.tensor_scalar_mul(rden[:, :], rden[:, :], col(C_XI)).then_inc(chain, 1)
                dve.wait_ge(chain, 6 * b + 2)
                for t in range(IT):
                    last = nc.vector.scalar_tensor_tensor(out=h[:, t, :], in0=O[t][:, D + 1:XC], scalar=rden[:, t:t + 1],
                                                          in1=xres[:, t, :], op0=ALU.mult, op1=ALU.add)
                last.then_inc(chain, 1)
                dve.wait_ge(chain, 6 * b + 3)
                for t in range(IT):
                    last = nc.vector.scalar_tensor_tensor(out=h[:, t, :], in0=O[t][:, 0:D], scalar=rden[:, t:t + 1],
                                                          in1=h[:, t, :], op0=ALU.mult, op1=ALU.add)
                last.then_inc(o_read, 1)
                dve.wait_ge(o_read, b + 1)
                layer_stats(lambda t: h[:, t, :], 0, 6 * b + 3)

            step(0, 0)
            with dve.Fori(1, NW) as w:
                step(0, w)
            with dve.Fori(1, NB) as b:
                step(b, 0, range(UT))
                rows(b - 1)
                step(b, 0, range(UT, UT + 1))
                norm_rows(b - 1)
                step(b, 0, range(UT + 1, WT))
                step(b, 1, range(1))
                split_sup(b - 1, slots_before(b) + WT + 1)
                step(b, 1, range(1, WT))
                with dve.Fori(2, NW) as w:
                    step(b, w)
            split_lo(NB * NT - 1, UT - 1)
            rows(NB - 1)
            norm_rows(NB - 1)
            split_sup(NB - 1, slots_before(NB) + 1)

            def widen(r, g):
                for s in (0, 2):
                    if not (r == 0 and isinstance(g, int)):
                        dve.wait_ge(agg_done, r * NT + g * 4 + s - 3)
                    nc.vector.tensor_copy(adjb[:, s, :].rearrange("p (b i) -> p b i", i=BI),
                                          adjT[:, 2 * r:2 * r + 2, g * 4 + s, :]).then_inc(adjb_v, 1)

            def finish(r):
                half = (r // 2) % 2
                dve.wait_ge(c_ready, r // 2 + 1)
                dve.wait_ge(x1_in[r % 2], 16 * (r // 2 + 1))
                base = 6 * NB + 4 * r
                st = stage[:, r % 2, :, :]
                for part in range(2):
                    for t in range(IT):
                        i = (r % 2) * IT + t
                        c = psum[:, CB[half] + i // 2, (i % 2) * 256 + (1 - part) * D:(i % 2) * 256 + (2 - part) * D]
                        src = st[:, t, 0:D] if part == 0 else st[:, t, D:2 * D]
                        last = nc.vector.scalar_tensor_tensor(out=st[:, t, D:2 * D], in0=c, scalar=col(C_SI),
                                                              in1=src, op0=ALU.mult, op1=ALU.add)
                    if part == 0:
                        last.then_inc(chain, 1)
                        dve.wait_ge(chain, base + 1)
                last.then_inc(c_read, 1)
                dve.wait_ge(c_read, r + 1)
                o = IT * (r % 2)
                layer_stats(lambda t: st[:, t, D:2 * D], o, base + 1)

            def normalise_y(r):
                st = stage[:, r % 2, :, :]
                normalise(lambda t: st[:, t, 2 * D:3 * D], lambda t: st[:, t, D:2 * D], IT * (r % 2),
                          NB + r + 1).then_inc(y_done, 1)

            dve.wait_ge(lo_done, NB * NT)
            dve.wait_ge(hi_done, NB * NT)
            widen(0, 0)
            for r in range(NB // 2):
                with dve.Fori(int(r == 0), NT // 4) as g:
                    widen(r, g)
                if r >= 1:
                    finish(2 * r - 2)
                    finish(2 * r - 1)
                    normalise_y(2 * r - 2)
                    normalise_y(2 * r - 1)
            finish(NB - 2)
            finish(NB - 1)
            normalise_y(NB - 2)
            normalise_y(NB - 1)



        @block.tensor
        def _(pe):
            pe.wait_ge(consts, 5)
            for g in range(NT // 4):
                pe.wait_ge(u_done, g + 1)
                if g >= 4:
                    pe.wait_ge(uT_lo, g - 3)
                for t in range(4):
                    last = nc.tensor.transpose(psum[:, g % 4, t * P:(t + 1) * P], work[:, 4 * g + t, :], ident[:, :])
                last.then_inc(uT_filled, 1)
            pe.wait_ge(pro, 4)
            nc.tensor.transpose(psum[0:NT, 4, 0:P], q[:, :], ident[:, :]).then_inc(q_filled, 1)
            pe.wait_ge(uT_lo, NT // 4)
            pe.wait_ge(q_moved, 1)
            pe.wait_ge(consts, 6)

            def masks(b, w, k):
                p = b * (NT // 2) + w * UT + k // 2
                s = k // UT
                if not (first(b, w) and k < 4):
                    pe.wait_ge(mask_stored, p - 1)
                if k % UT == 0:
                    pe.wait_ge(adj_in[s], (b * NW + w + 1) * 16)
                for kk in (k, k + 1):
                    for t in range(IT):
                        c = kk % UT
                        src = stage[:, s, t, c * P:(c + 1) * P].bitcast(BF16)[:, 1::2]
                        last = nc.tensor.transpose(T[(k // 2) % 2][:, kk % 2, t * P:(t + 1) * P], src, identb[:, :])
                last.then_inc(mask_filled, 1)

            def wait_slot(c):
                if not isinstance(c, int) or c >= 2:
                    pe.wait_ge(slot_done, c - 1)

            def scores(b, w, k):
                c = slot_of(b, w, k)
                wait_slot(c)
                j = (w * WT + k) * P
                i = b * BI
                o = S[bank_of(b, w, k)]
                hj, lj = uT[:, 0, bass.ds(j, P)], uT[:, 1, bass.ds(j, P)]
                hi, li = uT[:, 0, bass.ds(i, BI)], uT[:, 1, bass.ds(i, BI)]
                nc.tensor.matmul(o, hj, hi, start=True, stop=False)
                nc.tensor.matmul(o, hj, li, start=False, stop=False)
                nc.tensor.matmul(o, lj, hi, start=False, stop=True).then_inc(slot_filled, 1)

            def weigh(n, jt, k, stop=False):
                pe.wait_ge(lo_done, n + 1)
                for t in range(IT):
                    nc.tensor.matmul(O[t][:, 0:D + 1], el[:, k % UT, t * P:(t + 1) * P], xaug[:, jt, 0:D + 1],
                                     start=False, stop=False)
                    last = nc.tensor.matmul(O[t][:, 0:XC], eh[:, k % UT, t * P:(t + 1) * P], xaug[:, jt, :],
                                            start=False, stop=stop and k == UT - 1)
                last.then_inc(pv_done, 1)

            def clear():
                for t in range(IT):
                    nc.tensor.matmul(O[t][:, 0:XC], zeros[:, :], xaug[:, 0, :], start=True, stop=False)

            def step(b, w, weigh_first=True, ks=range(WT), stop=False):
                for k in ks:
                    if k % 2 == 0:
                        masks(b, w, k)
                    scores(b, w, k)
                    if weigh_first or k >= UT:
                        weigh(b * NT + w * WT + k - UT, (w * WT + k - UT) % NT if isinstance(w, int) else w * WT + k - UT,
                              k, stop)

            def rows_T(b, c, fourth):
                pe.wait_ge(x1_done, b + 1)
                wait_slot(c)
                for t in range(IT):
                    last = nc.tensor.transpose(S[0][:, t * P:(t + 1) * P], x1[:, t, :], ident[:, :])
                last.then_inc(slot_filled, 1)

            def sup(b, c):
                pe.wait_ge(slot_done, c)
                for t in range(IT):
                    last = nc.tensor.matmul(S[1][:, t * P:(t + 1) * P], x1T[:, t * P:(t + 1) * P], w_sb[:, :],
                                            start=True, stop=True)
                last.then_inc(slot_filled, 1)

            pe.wait_ge(pro, 17)
            pe.wait_ge(w_in, 16)
            step(0, 0, weigh_first=False, ks=range(UT))
            clear()
            step(0, 0, ks=range(UT, WT))
            with pe.Fori(1, NW) as w:
                step(0, w)
            with pe.Fori(1, NB) as b:
                step(b, 0, ks=range(UT), stop=True)
                pe.wait_ge(o_read, b)
                clear()
                step(b, 0, ks=range(UT, UT + 2))
                rows_T(b - 1, slots_before(b) + UT + 2, False)
                step(b, 0, ks=range(UT + 2, WT))
                sup(b - 1, slots_before(b) + WT + 1)
                with pe.Fori(1, NW) as w:
                    step(b, w)
            for k in range(UT):
                weigh(NB * NT - UT + k, NT - UT + k, k, stop=True)
            rows_T(NB - 1, slots_before(NB), False)
            sup(NB - 1, slots_before(NB) + 1)

            pe.wait_ge(sup_in, 16)
            for r in range(NB // 2):
                cb = CB[r % 2]
                if r == 0:
                    pe.wait_ge(o_read, NB)
                if r == 1:
                    pe.wait_ge(slot_done, slots_before(NB) + 2)
                if r >= 2:
                    pe.wait_ge(c_read, 2 * (r - 1))
                for i in range(4):
                    nc.tensor.matmul(psum[:, cb + i, :], zeros[:, :], sup_all[:, 0:2, :].rearrange("p a d -> p (a d)"),
                                     start=True, stop=False, skip_group_check=True)
                with pe.Fori(0, NT // 4) as g:
                    for s in range(4):
                        ready = adjb_v if s % 2 == 0 else adjb_a
                        pe.wait_ge(ready, r * (NT // 2) + g * 2 + s // 2 + 1)
                        for i in range(2 * IT):
                            last = nc.tensor.matmul(psum[:, cb + i // 2, (i % 2) * 256:(i % 2) * 256 + 256],
                                                    adjb[:, s, i * P:(i + 1) * P], sup_all[:, g * 4 + s, :],
                                                    start=False, stop=False, skip_group_check=True)
                        last.then_inc(agg_done, 1)
                for i in range(4):
                    last = nc.tensor.matmul(psum[:, cb + i, :], zeros[:, :], sup_all[:, 0:2, :].rearrange("p a d -> p (a d)"),
                                            start=False, stop=True, skip_group_check=True)
                last.then_inc(c_ready, 1)


def kernel(x, adj, L0_gnn_beta, L1_gnn_weight):
    import numpy as np
    import concourse.bacc as bacc
    from concourse.bass_utils import run_bass_kernel_spmd

    nc = bacc.Bacc("TRN2", target_bir_lowering=False, num_devices=1)
    N, D = x.shape
    arrays = {"in_x": x, "in_adj": adj, "in_beta": L0_gnn_beta, "in_weight": L1_gnn_weight}
    arrays = {k: np.ascontiguousarray(v) for k, v in arrays.items()}
    aps = [nc.dram_tensor(k, v.shape, mybir.dt.from_np(v.dtype), kind="ExternalInput").ap() for k, v in arrays.items()]
    x1_dram = nc.dram_tensor("x1_rows", (N, D), F32).ap()
    sup_dram = nc.dram_tensor("support_parts", (N, 2 * D), F16).ap()
    q_dram = nc.dram_tensor("norms", (1, N), F32).ap()
    out = nc.dram_tensor("out", (N, D), F32, kind="ExternalOutput").ap()
    resnorm_graph_kernel(nc, *aps, x1_dram, sup_dram, q_dram, out)
    return run_bass_kernel_spmd(nc, [arrays], core_ids=[0]).results[0]["out"]
```

```python
from contextlib import ExitStack

import concourse.bass as bass
from concourse import mybir

F32 = mybir.dt.float32
F16 = mybir.dt.float16
BF16 = mybir.dt.bfloat16
U8 = mybir.dt.uint8
I32 = mybir.dt.int32
ALU = mybir.AluOpType
ACT = mybir.ActivationFunctionType
AX = mybir.AxisListType
RMAX = bass.bass_isa.ReduceOp.max
RADD = bass.bass_isa.ReduceOp.add

P = 128
EPS_LN = 1e-5
EPS_COS = 1e-7


def resnorm_graph_kernel(nc, x, adj, beta, weight, x1_dram, sup_dram, q_dram, out):
    N, D = x.shape
    BI = 512
    NB = N // BI
    IT = BI // P
    NT = N // P
    UT = 4
    NU = NT // UT
    WT = 2 * UT
    NW = NT // WT
    XC = 2 * D + 1
    ESC = 2.0 ** 15
    USC = 2.0 ** 15
    assert D == P and NB % 2 == 0 and NW > 1

    with ExitStack() as ctx:
        def sb(name, shape, dt):
            return ctx.enter_context(nc.sbuf_tensor(name, shape, dt))

        def sem(name):
            return ctx.enter_context(nc.semaphore(name))

        adjT = sb("adjT", [P, NB, NT, BI], U8)
        stage = sb("stage", [P, 2, IT, UT * P], F32)
        uT = sb("uT", [P, 2, N], F16)
        xaug = sb("xaug", [P, NT, XC], F16)
        E = sb("E", [P, UT, BI], F32)
        eh = sb("eh", [P, UT, BI], F16)
        el = sb("el", [P, UT, BI], F16)
        xres = sb("xres", [P, IT, D], F32)
        raw = sb("raw", [P, IT, XC], F32)
        sup32 = sb("sup32", [P, IT, D], F32)
        h = raw[:, :, D + 1:XC]
        x1 = raw[:, :, 0:D]
        x1T = sup32[:, :, :].rearrange("p t d -> p (t d)")
        q_row = sb("q_row", [P, BI], F32)
        q_T = sb("q_T", [NT, P], F32)
        flag = sb("flag", [P, 1], I32)
        sup2 = sb("sup2", [P, IT, 2, D], F16)
        w_sb = sb("w_sb", [P, D], F32)
        ident = sb("ident", [P, P], F32)
        identb = sb("identb", [P, P], BF16)
        zeros = sb("zeros", [P, P], F16)
        n2 = sb("n2", [P, NT], F32)
        rn = sb("rn", [P, NT], F32)
        q = sb("q", [P, NT], F32)
        rnu = sb("rnu", [P, NT], F32)
        half_pow = sb("half_pow", [P, NT], F32)
        sc = sb("sc", [P, 17], F32)
        stats = sb("stats", [P, 8, 6], F32)
        mean = sb("mean", [P, 8], F32)
        tmp = sb("tmp", [P, 3, 8], F32)
        rstd = sb("rstd", [P, 8], F32)
        rden = sb("rden", [P, IT], F32)

        xfull = adjT[:, NB - 1, :, :].rearrange("p t i -> p (t i)").bitcast(F32).rearrange("p (t d) -> p t d", d=D)
        work = adjT[:, NB - 2, :, :].rearrange("p t i -> p (t i)").bitcast(F32).rearrange("p (t d) -> p t d", d=D)
        xsc = adjT[:, NB - 3, :, :].rearrange("p t i -> p (t i)").bitcast(F32).rearrange("p (t d) -> p t d", d=D)
        sup_all = uT[:, :, :].rearrange("p a (t d) -> p (a t) d", d=2 * D)
        sup_last = sup_all[:, NT - IT:NT, :].rearrange("p t (a d) -> p t a d", d=D)
        adjb = [part.rearrange("p a i -> p (a i)").bitcast(BF16).rearrange("p (s t i) -> p s t i", t=2, i=BI)[:, s]
                for part, n in ((E[:, :, :], UT), (eh[:, :, :], UT // 2), (el[:, :, :], UT // 2)) for s in range(n)]
        NS = len(adjb)
        NR = NT // 2
        M_ROWS_T, M_SUP = 8, 12

        C_RMAX, C_QMAX, C_FRO, C_G0, C_G1, C_G2 = 0, 1, 2, 3, 4, 5
        C_PX, C_PF, C_XS, C_XI, C_SS, C_SI, C_B, C_BS, C_BB, C_T, C_T2 = range(6, 17)

        def col(c):
            return sc[:, c:c + 1]

        psum = ctx.enter_context(nc.psum_tensor("psum", [P, 8, 512], F32))
        S = [psum[:, b, :] for b in range(2)]
        T = [psum[:, 2 + b, :].bitcast(BF16).rearrange("p (t i) -> p t i", i=BI) for b in range(2)]
        O = [psum[:, 4 + b, :] for b in range(IT)]

        CB = [4, 6]

        x_in = sem("x_in")
        w_in = sem("w_in")
        beta_in = sem("beta_in")
        adj_in = [sem(f"adj_in{b}") for b in range(2)]
        xres_in = sem("xres_in")
        consts = sem("consts")
        q_filled = sem("q_filled")
        q_moved = sem("q_moved")
        q_stored = sem("q_stored")
        q_row_in = sem("q_row_in")
        flag_set = sem("flag_set")
        half_scaled = sem("half_scaled")
        scaled = sem("scaled")
        fix = sem("fix")
        pro = sem("pro")
        gp = sem("gp")
        uT_filled = sem("uT_filled")
        uT_hi = sem("uT_hi")
        uT_lo = sem("uT_lo")
        slot_filled = sem("slot_filled")
        slot_done = sem("slot_done")
        mask_filled = sem("mask_filled")
        mask_stored = sem("mask_stored")
        masked = sem("masked")
        hi_v = sem("hi_v")
        hi_a = sem("hi_a")
        lo_done = sem("lo_done")
        pv_done = sem("pv_done")
        o_read_v = sem("o_read_v")
        o_read_a = sem("o_read_a")
        chain = sem("chain")
        stats_done = sem("stats_done")
        rstd_done = sem("rstd_done")
        x1_done = sem("x1_done")
        x1_stored = sem("x1_stored")
        sup_hi = sem("sup_hi")
        sup_split = sem("sup_split")
        u_done = sem("u_done")
        sup_stored = sem("sup_stored")
        sup_in = [sem(f"sup_in{g}") for g in range(4)]
        adjb_v = sem("adjb_v")
        adjb_a = sem("adjb_a")
        agg_done = sem("agg_done")
        c_read = sem("c_read")
        x1_in = [sem(f"x1_in{b}") for b in range(2)]
        y_done = sem("y_done")
        y_stored = [sem(f"y_stored{b}") for b in range(2)]

        adj_v = adj.rearrange("(b t p) (u c) -> b u p t c", p=P, t=IT, c=UT * P)
        x_v = x.rearrange("(b t p) d -> b p t d", p=P, t=IT)
        x1_v = x1_dram.rearrange("(b t p) d -> b p t d", p=P, t=IT)
        sup_v = sup_dram.rearrange("(b t p) d -> b p t d", p=P, t=IT)
        sup_l = sup_dram.rearrange("(t p) d -> p t d", p=P)
        q_v = q_dram.rearrange("a (t p) -> (a t) p", p=P)
        out_v = out.rearrange("(b t p) d -> b p t d", p=P, t=IT)

        block = ctx.enter_context(nc.Block())

        def slots_before(b):
            return b * (NT + 2) - 2

        def slot_rows_T(b):
            return slots_before(b + 1) + (NW - 1) * WT if not (isinstance(b, int) and b == NB - 1) else slots_before(NB)

        def slot_sup(b):
            return slot_rows_T(b) + (1 + UT if not (isinstance(b, int) and b == NB - 1) else 1)

        def slot_shift(b, w, k):
            if isinstance(b, int) and b == 0 or not (isinstance(w, int) and w == NW - 1):
                return 0
            return 1 if k < UT else 2

        def slot_of(b, w, k):
            before = 0 if isinstance(b, int) and b == 0 else slots_before(b)
            return before + w * WT + k + slot_shift(b, w, k)

        def bank_of(b, w, k):
            return (k + slot_shift(b, w, k)) % 2

        def first(b, w):
            return isinstance(b, int) and b == 0 and isinstance(w, int) and w == 0

        @block.sync
        def _(sp):
            for c in range(4):
                s = slice(c * NT // 4, (c + 1) * NT // 4)
                sp.dma_start(xfull[:, s, :], x.rearrange("(t p) d -> p t d", p=P)[:, s, :]).then_inc(x_in, 16)
            sp.dma_start(w_sb[:, :], weight).then_inc(w_in, 16)
            sp.dma_start(col(C_B), beta.rearrange("(a b) -> a b", a=1).to_broadcast([P, 1])).then_inc(beta_in, 16)

            def load_unit(b, u, slot):
                sp.dma_start(stage[:, slot, :, :], adj_v[b, u, :, :, :]).then_inc(adj_in[slot], 16)

            def load_units(b, w):
                for s in range(2):
                    if not first(b, w):
                        sp.wait_ge(mask_filled, (b * NU + 2 * w + s - 1) * 2)
                    load_unit(b, 2 * w + s, s)

            def store_x1(b):
                sp.wait_ge(x1_done, b + 1)
                sp.dma_start(x1_v[b], x1[:, :, :]).then_inc(x1_stored, 16)

            def load_xres(b):
                sp.dma_start(xres[:, :, :], x_v[b]).then_inc(xres_in, 16)

            def load_q_row(b):
                if not isinstance(b, int) or b > 0:
                    sp.wait_ge(masked, NT * b)
                sp.dma_start(q_row[:, :], q_dram[0:1, bass.ds(b * BI, BI)].to_broadcast([P, BI])).then_inc(q_row_in, 16)

            load_xres(0)
            load_units(0, 0)
            sp.wait_ge(q_moved, 1)
            sp.dma_start(q_v, q_T[:, :]).then_inc(q_stored, 16)
            sp.wait_ge(q_stored, 16)
            load_q_row(0)
            with sp.Fori(1, NW) as w:
                load_units(0, w)
            with sp.Fori(1, NB) as b:
                load_units(b, 0)
                load_q_row(b)
                load_units(b, 1)
                store_x1(b - 1)
                load_xres(b)
                with sp.Fori(2, NW) as w:
                    load_units(b, w)
            sp.wait_ge(slot_filled, slots_before(NB))
            sp.wait_ge(sup_stored, 16 * (NB - 1))
            for g in range(4):
                s = slice(g * NT // 4, min((g + 1) * NT // 4, NT - IT))
                sp.dma_start(sup_all[:, s, :], sup_l[:, s, :]).then_inc(sup_in[g], 16)
            store_x1(NB - 1)
            sp.wait_ge(x1_stored, 16 * NB)

            def load_x1(r, slot):
                sp.dma_start(stage[:, slot, :, 0:D], x1_v[r]).then_inc(x1_in[slot], 16)

            def store_y(r, slot):
                sp.wait_ge(y_done, r + 1)
                sp.dma_start(out_v[r], stage[:, slot, :, 2 * D:3 * D]).then_inc(y_stored[slot], 16)

            load_x1(0, 0)
            load_x1(1, 1)
            with sp.Fori(1, NB // 2) as rr:
                for s in range(2):
                    store_y(rr * 2 + s - 2, s)
                    sp.wait_ge(y_stored[s], rr * 16)
                    load_x1(rr * 2 + s, s)
            store_y(NB - 2, 0)
            store_y(NB - 1, 1)
            sp.wait_ge(y_stored[0], 8 * NB)
            sp.wait_ge(y_stored[1], 8 * NB)

        @block.gpsimd
        def _(pool):
            nc.gpsimd.memset(ident[:, :], 0.0).then_inc(consts, 1)
            nc.gpsimd.memset(zeros[:, :], 0.0).then_inc(consts, 1)
            nc.gpsimd.memset(xaug[:, :, D:D + 1], 1.0).then_inc(consts, 1)
            nc.gpsimd.memset(half_pow[:, :], -0.5).then_inc(consts, 1)
            pool.wait_ge(consts, 4)
            nc.gpsimd.affine_select(out=ident[:, :], in_=ident[:, :], compare_op=ALU.not_equal, fill=1.0,
                                    base=0, pattern=[[-1, P]], channel_multiplier=1).then_inc(consts, 1)
            pool.wait_ge(consts, 5)
            nc.gpsimd.tensor_copy(identb[:, :], ident[:, :]).then_inc(consts, 1)
            pool.wait_ge(pro, 3)
            nc.gpsimd.tensor_tensor(rn[:, :], n2[:, :], half_pow[:, :], ALU.pow).then_inc(gp, 1)
            pool.wait_ge(pro, 7)
            nc.gpsimd.partition_all_reduce(sc[:, C_G0:C_G0 + 2], sc[:, C_RMAX:C_RMAX + 2], P, RMAX).then_inc(gp, 1)
            nc.gpsimd.partition_all_reduce(col(C_G2), col(C_FRO), P, RADD).then_inc(gp, 1)

            def rsqrt_rows(done, c):
                pool.wait_ge(stats_done, done)
                nc.gpsimd.tensor_tensor(rstd[:, c:c + IT], rstd[:, c:c + IT], half_pow[:, 0:IT],
                                        ALU.pow).then_inc(rstd_done, 1)

            with pool.Fori(1, NB + 1) as b:
                rsqrt_rows(b, 0)
            for r in range(NB):
                rsqrt_rows(NB + r + 1, IT * (r % 2))

        @block.scalar
        def _(act):
            for g in range(NT // 4):
                act.wait_ge(uT_filled, g + 1)
                nc.scalar.activation(uT[:, 0, g * 512:(g + 1) * 512], psum[:, g % 4, :], ACT.Copy).then_inc(uT_hi, 1)
            act.wait_ge(q_filled, 1)
            nc.scalar.activation(q_T[:, :], psum[0:NT, 4, 0:P], ACT.Copy).then_inc(q_moved, 1)
            act.wait_ge(pro, 10)
            act.wait_ge(flag_set, 1)
            small = act.value_load(flag[0:1, 0:1], min_val=0, max_val=1)

            def exp_tile(b, w, k):
                c = slot_of(b, w, k)
                n = b * NT + w * WT + k
                act.wait_ge(slot_filled, c + 1)
                act.wait_ge(scaled, (n + 1) * small + 1)
                if not (first(b, w) and k < UT):
                    act.wait_ge(lo_done, n - UT + 1)
                nc.scalar.activation(E[:, k % UT, :], S[bank_of(b, w, k)], ACT.Exp,
                                     bias=col(C_BB), scale=col(C_BS)).then_inc(slot_done, 1)

            def store_masks(b, w, k):
                p = (b * NT + w * WT + k) // 2 if isinstance(b, int) and isinstance(w, int) else b * (NT // 2) + w * UT + k // 2
                act.wait_ge(mask_filled, p + 1)
                nc.scalar.activation(adjT[:, b, bass.ds(w * WT + k, 2), :], T[(k // 2) % 2], ACT.Copy).then_inc(mask_stored, 1)

            def rows_T(b):
                act.wait_ge(slot_filled, slot_rows_T(b) + 1)
                if not isinstance(b, int) or b > 0:
                    act.wait_ge(sup_split, b)
                nc.scalar.activation(x1T, S[0], ACT.Copy).then_inc(slot_done, 1)

            def sup_out(b):
                act.wait_ge(slot_filled, slot_sup(b) + 1)
                nc.scalar.activation(sup32[:, :, :].rearrange("p t d -> p (t d)"), S[1], ACT.Copy,
                                     scale=col(C_SS)).then_inc(slot_done, 1)

            def store_sup(b):
                act.wait_ge(sup_split, b + 1)
                act.dma_start(sup_v[b], sup2[:, :, :, :].rearrange("p t a d -> p t (a d)")).then_inc(sup_stored, 16)

            def read_out(b):
                act.wait_ge(pv_done, (b + 1) * NT)
                if not isinstance(b, int) or b > 0:
                    act.wait_ge(x1_stored, 16 * b)
                nc.scalar.activation(raw[:, IT // 2:IT, :], psum[:, 4 + IT // 2:4 + IT, 0:XC], ACT.Copy).then_inc(o_read_a, 1)

            def split_hi(b, w, k):
                n = b * NT + w * WT + k
                act.wait_ge(masked, n + 1)
                if not (first(b, w) and k < UT):
                    act.wait_ge(pv_done, n - UT + 1)
                nc.scalar.activation(eh[:, k % UT, :], E[:, k % UT, :], ACT.Copy).then_inc(hi_a, 1)

            def step(b, w, ks=range(0, WT, 2)):
                for k in ks:
                    store_masks(b, w, k)
                    exp_tile(b, w, k)
                    if not (first(b, w) and k == 0):
                        split_hi(b, w, k - 1)
                    exp_tile(b, w, k + 1)

            step(0, 0)
            with act.Fori(1, NW) as w:
                step(0, w)
            with act.Fori(1, NB) as b:
                step(b, 0, range(0, UT, 2))
                read_out(b - 1)
                step(b, 0, range(UT, WT, 2))
                with act.Fori(1, NW - 1) as w:
                    step(b, w)
                rows_T(b - 1)
                step(b, NW - 1, range(0, UT, 2))
                sup_out(b - 1)
                step(b, NW - 1, range(UT, WT, 2))
                store_sup(b - 1)
            split_hi(NB - 1, NW, -1)
            read_out(NB - 1)

            def widen(r, m):
                if not (isinstance(r, int) and r == 0 and m < NS):
                    act.wait_ge(agg_done, r * NR + m - NS + 1)
                nc.scalar.activation(adjb[m % NS], adjT[:, r, 2 * m:2 * m + 2, :], ACT.Copy).then_inc(adjb_a, 1)

            act.wait_ge(lo_done, NB * NT)
            act.wait_ge(pv_done, NB * NT)
            for m in range(1, NR, 2):
                widen(0, m)
                if m == M_ROWS_T + 1:
                    rows_T(NB - 1)
                if m == M_SUP + 1:
                    sup_out(NB - 1)
            with act.Fori(1, NB) as r:
                for m in range(1, NR, 2):
                    widen(r, m)

        @block.vector
        def _(dve):
            dve.wait_ge(x_in, 64)
            nc.vector.tensor_tensor(work, xfull, xfull, ALU.mult).then_inc(pro, 1)
            dve.wait_ge(pro, 1)
            nc.vector.tensor_reduce(n2[:, :], work, op=ALU.add, axis=AX.X).then_inc(pro, 1)
            dve.wait_ge(pro, 2)
            nc.vector.tensor_scalar_max(n2[:, :], n2[:, :], 1e-36).then_inc(pro, 1)
            dve.wait_ge(gp, 1)
            nc.vector.reciprocal(q[:, :], rn[:, :]).then_inc(pro, 1)
            nc.vector.reduce_max(col(C_RMAX), rn[:, :], AX.X).then_inc(pro, 1)
            dve.wait_ge(pro, 4)
            nc.vector.reduce_max(col(C_QMAX), q[:, :], AX.X).then_inc(pro, 1)
            dve.wait_ge(w_in, 16)
            nc.vector.tensor_tensor_reduce(out=raw[:, 0, 0:D], in0=w_sb[:, :], in1=w_sb[:, :], scale=1.0, scalar=0.0,
                                           op0=ALU.mult, op1=ALU.add, accum_out=col(C_FRO)).then_inc(pro, 1)
            nc.vector.tensor_scalar_mul(rnu[:, :], rn[:, :], USC).then_inc(pro, 1)
            dve.wait_ge(pro, 8)
            for t in range(NT):
                last = nc.vector.tensor_scalar_mul(work[:, t, :], xfull[:, t, :], rnu[:, t:t + 1])
                if t % 4 == 3:
                    last.then_inc(u_done, 1)
            dve.wait_ge(beta_in, 16)
            nc.vector.tensor_scalar_mul(col(C_BS), col(C_B), 1.0 / (USC * USC)).then_inc(pro, 1)
            nc.vector.tensor_scalar(col(C_BB), col(C_B), -1.0, col(C_B), ALU.mult, ALU.min).then_inc(pro, 1)
            dve.wait_ge(gp, 3)
            nc.vector.tensor_scalar(sc[:, C_PX:C_PX + 1].bitcast(I32), col(C_G1).bitcast(I32), 0x7F800000, None,
                                    ALU.bitwise_and).then_inc(pro, 1)
            nc.vector.tensor_scalar(sc[:, C_PF:C_PF + 1].bitcast(I32), col(C_G2).bitcast(I32), 0x7F800000, None,
                                    ALU.bitwise_and).then_inc(pro, 1)
            dve.wait_ge(pro, 12)
            nc.vector.reciprocal(col(C_XS), col(C_PX)).then_inc(pro, 1)
            nc.vector.tensor_scalar_mul(col(C_XI), col(C_PX), 2.0 ** -14).then_inc(pro, 1)
            dve.wait_ge(pro, 14)
            nc.vector.tensor_scalar(xsc, xfull, col(C_XS), 2.0 ** 14, ALU.mult, ALU.mult).then_inc(pro, 1)
            dve.wait_ge(pro, 15)
            nc.vector.tensor_copy(xaug[:, :, 0:D], xsc).then_inc(pro, 1)
            dve.wait_ge(pro, 16)
            nc.vector.tensor_tensor(xaug[:, :, D + 1:XC], xsc, xaug[:, :, 0:D], ALU.subtract).then_inc(pro, 1)
            nc.vector.tensor_scalar_max(col(C_T), col(C_PF), 1e-30).then_inc(pro, 1)
            dve.wait_ge(pro, 18)
            nc.vector.reciprocal(col(C_SS), col(C_T)).then_inc(pro, 1)
            nc.vector.tensor_scalar_mul(col(C_SI), col(C_T), 1.0).then_inc(pro, 1)
            dve.wait_ge(gp, 3)
            nc.vector.tensor_tensor(col(C_T2), col(C_G0), col(C_G0), ALU.mult).then_inc(fix, 1)
            dve.wait_ge(fix, 1)
            nc.vector.tensor_scalar(flag[:, :], col(C_T2), 0.5, None, ALU.is_gt).then_inc(flag_set, 1)
            dve.wait_ge(flag_set, 1)
            nc.vector.tensor_copy(col(C_T2), flag[:, :]).then_inc(scaled, 1)
            small = dve.value_load(flag[0:1, 0:1], min_val=0, max_val=1)
            for g in range(NT // 4):
                dve.wait_ge(uT_hi, g + 1)
                nc.vector.tensor_tensor(uT[:, 1, g * 512:(g + 1) * 512], psum[:, g % 4, :],
                                        uT[:, 0, g * 512:(g + 1) * 512], ALU.subtract).then_inc(uT_lo, 1)

            HB = BI // 2

            def add_small_term(b, w, k):
                n = b * NT + w * WT + k
                dve.wait_ge(slot_filled, slot_of(b, w, k) + 1)
                dve.wait_ge(q_row_in, 16 * (b + 1))
                if not (first(b, w) and k < UT):
                    dve.wait_ge(lo_done, n - UT + 1)
                num, den = E[:, k % UT, 0:HB], E[:, k % UT, HB:BI]
                s = S[bank_of(b, w, k)]
                for half in range(2):
                    base = 1 + 8 * n + 4 * half
                    part = slice(half * HB, (half + 1) * HB)
                    nc.vector.tensor_scalar_mul(num, q_row[:, part], q[:, bass.ds(w * WT + k, 1)]).then_inc(fix, 1)
                    dve.wait_ge(fix, base + 1)
                    nc.vector.tensor_scalar_add(den, num, EPS_COS).then_inc(fix, 1)
                    dve.wait_ge(fix, base + 2)
                    nc.vector.reciprocal(den, den).then_inc(fix, 1)
                    dve.wait_ge(fix, base + 3)
                    nc.vector.tensor_tensor(num, num, den, ALU.mult).then_inc(fix, 1)
                    dve.wait_ge(fix, base + 4)
                    done = nc.vector.tensor_tensor(s[:, part], s[:, part], num, ALU.mult)
                    done.then_inc(half_scaled, 1) if half == 0 else done.then_inc(scaled, 1)
                    if half == 0:
                        dve.wait_ge(half_scaled, n + 1)

            def mask_tile(b, w, k):
                n = b * NT + w * WT + k
                with dve.If(small > 0):
                    add_small_term(b, w, k)
                p = b * (NT // 2) + w * UT + k // 2
                dve.wait_ge(slot_done, slot_of(b, w, k) + 1)
                dve.wait_ge(mask_stored, p + 1)
                nc.vector.scalar_tensor_tensor(out=E[:, k % UT, :], in0=E[:, k % UT, :], scalar=ESC,
                                               in1=adjT[:, b, w * WT + k, :], op0=ALU.mult,
                                               op1=ALU.mult).then_inc(masked, 1)

            def split_hi(b, w, k):
                n = b * NT + w * WT + k
                dve.wait_ge(masked, n + 1)
                if not (first(b, w) and k < UT):
                    dve.wait_ge(pv_done, n - UT + 1)
                nc.vector.tensor_copy(eh[:, k % UT, :], E[:, k % UT, :]).then_inc(hi_v, 1)

            def split_lo(b, w, k):
                half = b * (NT // 2) + w * (WT // 2)
                dve.wait_ge(hi_v if k % 2 == 0 else hi_a, half + (k // 2 + 1 if k > 0 else 1 if k == 0 else 0))
                nc.vector.tensor_tensor(el[:, k % UT, :], E[:, k % UT, :], eh[:, k % UT, :],
                                        ALU.subtract).then_inc(lo_done, 1)

            def step(b, w, ks=range(0, WT, 2), amid=None):
                for k in ks:
                    mask_tile(b, w, k)
                    if amid and k == UT - 2:
                        amid()
                    split_hi(b, w, k)
                    if not (first(b, w) and k == 0):
                        split_lo(b, w, k - 1)
                    mask_tile(b, w, k + 1)
                    split_lo(b, w, k)

            def layer_stats(src, o, base):
                for t in range(IT):
                    last = nc.vector.bn_stats(stats[:, o + t, :], src(t))
                last.then_inc(chain, 1)
                dve.wait_ge(chain, base + 1)
                s_ = slice(o, o + IT)
                nc.vector.tensor_tensor(tmp[:, 0, s_], stats[:, s_, 1], stats[:, s_, 4], ALU.add)
                nc.vector.tensor_tensor(tmp[:, 1, s_], stats[:, s_, 1], stats[:, s_, 4], ALU.subtract)
                nc.vector.tensor_tensor(tmp[:, 2, s_], stats[:, s_, 2], stats[:, s_, 5], ALU.add).then_inc(chain, 1)
                dve.wait_ge(chain, base + 2)
                nc.vector.tensor_scalar(tmp[:, 2, s_], tmp[:, 2, s_], 1.0 / D, EPS_LN, ALU.mult, ALU.add)
                nc.vector.scalar_tensor_tensor(out=tmp[:, 1, s_], in0=tmp[:, 1, s_], scalar=0.25, in1=tmp[:, 1, s_],
                                               op0=ALU.mult, op1=ALU.mult)
                nc.vector.tensor_scalar_mul(mean[:, s_], tmp[:, 0, s_], 0.5).then_inc(chain, 1)
                dve.wait_ge(chain, base + 3)
                nc.vector.tensor_tensor(rstd[:, s_], tmp[:, 1, s_], tmp[:, 2, s_], ALU.add).then_inc(stats_done, 1)

            def normalise(dst, src, o, done):
                dve.wait_ge(rstd_done, done)
                for t in range(IT):
                    last = nc.vector.tensor_scalar(dst(t), src(t), mean[:, o + t:o + t + 1],
                                                   rstd[:, o + t:o + t + 1], ALU.subtract, ALU.mult)
                return last

            def norm_rows(b):
                normalise(lambda t: x1[:, t, :], lambda t: h[:, t, :], 0, b + 1).then_inc(x1_done, 1)

            def split_sup(b):
                dve.wait_ge(slot_done, slot_sup(b) + 1)
                if not isinstance(b, int) or b > 0:
                    dve.wait_ge(sup_stored, 16 * b)
                dst = sup_last if isinstance(b, int) and b == NB - 1 else sup2
                nc.vector.tensor_copy(dst[:, :, 0, :], sup32[:, :, :]).then_inc(sup_hi, 1)
                dve.wait_ge(sup_hi, b + 1)
                nc.vector.tensor_tensor(dst[:, :, 1, :], sup32[:, :, :], dst[:, :, 0, :],
                                        ALU.subtract).then_inc(sup_split, 1)

            def read_out(b):
                dve.wait_ge(pv_done, (b + 1) * NT)
                if not isinstance(b, int) or b > 0:
                    dve.wait_ge(x1_stored, 16 * b)
                nc.vector.tensor_copy(raw[:, 0:IT // 2, :], psum[:, 4:4 + IT // 2, 0:XC]).then_inc(o_read_v, 1)

            def rows(b):
                dve.wait_ge(o_read_v, b + 1)
                dve.wait_ge(o_read_a, b + 1)
                dve.wait_ge(xres_in, 16 * (b + 1))
                nc.vector.reciprocal(rden[:, :], raw[:, :, D])
                nc.vector.tensor_tensor(h, x1, h, ALU.add).then_inc(chain, 1)
                dve.wait_ge(chain, 6 * b + 1)
                nc.vector.tensor_scalar_mul(rden[:, :], rden[:, :], col(C_XI)).then_inc(chain, 1)
                dve.wait_ge(chain, 6 * b + 2)
                for t in range(IT):
                    last = nc.vector.scalar_tensor_tensor(out=h[:, t, :], in0=h[:, t, :], scalar=rden[:, t:t + 1],
                                                          in1=xres[:, t, :], op0=ALU.mult, op1=ALU.add)
                last.then_inc(chain, 1)
                dve.wait_ge(chain, 6 * b + 3)
                layer_stats(lambda t: h[:, t, :], 0, 6 * b + 3)

            step(0, 0)
            with dve.Fori(1, NW) as w:
                step(0, w)
            with dve.Fori(1, NB) as b:
                step(b, 0, range(0, UT, 2), amid=lambda: read_out(b - 1))
                step(b, 0, range(UT, UT + 2, 2))
                rows(b - 1)
                step(b, 0, range(UT + 2, WT, 2))
                norm_rows(b - 1)
                with dve.Fori(1, NW - 1) as w:
                    step(b, w)
                step(b, NW - 1, range(0, UT + 2, 2))
                split_sup(b - 1)
                step(b, NW - 1, range(UT + 2, WT, 2))
            split_lo(NB - 1, NW, -1)
            read_out(NB - 1)

            def widen(r, m):
                if not (isinstance(r, int) and r == 0 and m < NS):
                    dve.wait_ge(agg_done, r * NR + m - NS + 1)
                elif m == 0:
                    dve.wait_ge(lo_done, NB * NT)
                elif m == UT:
                    dve.wait_ge(pv_done, NB * NT)
                nc.vector.tensor_copy(adjb[m % NS], adjT[:, r, 2 * m:2 * m + 2, :]).then_inc(adjb_v, 1)

            def add_part(r, slot, part):
                base = 6 * NB + 4 * r
                st = stage[:, slot, :, :]
                if part == 0:
                    dve.wait_ge(agg_done, (r + 1) * NR)
                    dve.wait_ge(x1_in[slot], 16 * (r // 2 + 1) if isinstance(r, int) else 8 * (r - slot) + 16)
                else:
                    dve.wait_ge(chain, base + 1)
                for t in range(IT):
                    c = psum[:, CB[slot] + t // 2, (t % 2) * 256 + (1 - part) * D:(t % 2) * 256 + (2 - part) * D]
                    src = st[:, t, 0:D] if part == 0 else st[:, t, D:2 * D]
                    last = nc.vector.scalar_tensor_tensor(out=st[:, t, D:2 * D], in0=c, scalar=col(C_SI),
                                                          in1=src, op0=ALU.mult, op1=ALU.add)
                last.then_inc(c_read if part else chain, 1)

            def y_stats(r, slot):
                dve.wait_ge(c_read, r + 1)
                layer_stats(lambda t: stage[:, slot, t, D:2 * D], IT * slot, 6 * NB + 4 * r + 1)

            def normalise_y(r, slot):
                st = stage[:, slot, :, :]
                normalise(lambda t: st[:, t, 2 * D:3 * D], lambda t: st[:, t, D:2 * D], IT * slot,
                          NB + r + 1).then_inc(y_done, 1)

            rows(NB - 1)
            for m in range(0, NR, 2):
                widen(0, m)
                if m == 2:
                    norm_rows(NB - 1)
                if m == M_SUP:
                    split_sup(NB - 1)

            def round_(r, slot):
                for m in range(0, NR, 2):
                    widen(r, m)
                    if m < 4:
                        add_part(r - 1, 1 - slot, m // 2)
                    if m == 4:
                        y_stats(r - 1, 1 - slot)
                    if m == 8:
                        normalise_y(r - 1, 1 - slot)

            with dve.Fori(0, NB // 2 - 1) as rr:
                round_(rr * 2 + 1, 1)
                round_(rr * 2 + 2, 0)
            round_(NB - 1, 1)
            add_part(NB - 1, 1, 0)
            add_part(NB - 1, 1, 1)
            y_stats(NB - 1, 1)
            normalise_y(NB - 1, 1)

        @block.tensor
        def _(pe):
            pe.wait_ge(consts, 5)
            for g in range(NT // 4):
                pe.wait_ge(u_done, g + 1)
                if g >= 4:
                    pe.wait_ge(uT_lo, g - 3)
                for t in range(4):
                    last = nc.tensor.transpose(psum[:, g % 4, t * P:(t + 1) * P], work[:, 4 * g + t, :], ident[:, :])
                last.then_inc(uT_filled, 1)
            pe.wait_ge(pro, 4)
            nc.tensor.transpose(psum[0:NT, 4, 0:P], q[:, :], ident[:, :]).then_inc(q_filled, 1)
            pe.wait_ge(uT_lo, NT // 4)
            pe.wait_ge(q_moved, 1)
            pe.wait_ge(consts, 6)

            def masks(b, w, k):
                p = b * (NT // 2) + w * UT + k // 2
                s = k // UT
                if not (first(b, w) and k < 4):
                    pe.wait_ge(mask_stored, p - 1)
                if k % UT == 0:
                    pe.wait_ge(adj_in[s], (b * NW + w + 1) * 16)
                for kk in (k, k + 1):
                    for t in range(IT):
                        c = kk % UT
                        src = stage[:, s, t, c * P:(c + 1) * P].bitcast(BF16)[:, 1::2]
                        last = nc.tensor.transpose(T[(k // 2) % 2][:, kk % 2, t * P:(t + 1) * P], src, identb[:, :])
                last.then_inc(mask_filled, 1)

            def wait_slot(c):
                if not isinstance(c, int) or c >= 2:
                    pe.wait_ge(slot_done, c - 1)

            def scores(b, w, k):
                c = slot_of(b, w, k)
                wait_slot(c)
                j = (w * WT + k) * P
                i = b * BI
                o = S[bank_of(b, w, k)]
                hj, lj = uT[:, 0, bass.ds(j, P)], uT[:, 1, bass.ds(j, P)]
                hi, li = uT[:, 0, bass.ds(i, BI)], uT[:, 1, bass.ds(i, BI)]
                nc.tensor.matmul(o, hj, hi, start=True, stop=False)
                nc.tensor.matmul(o, hj, li, start=False, stop=False)
                nc.tensor.matmul(o, lj, hi, start=False, stop=True).then_inc(slot_filled, 1)

            def weigh(n, jt, k, start=False, stop=False):
                pe.wait_ge(lo_done, n + 1)
                for t in range(IT):
                    def hi():
                        return nc.tensor.matmul(O[t][:, 0:XC], eh[:, k % UT, t * P:(t + 1) * P], xaug[:, jt, :],
                                                start=start, stop=stop)

                    def lo():
                        return nc.tensor.matmul(O[t][:, 0:D + 1], el[:, k % UT, t * P:(t + 1) * P],
                                                xaug[:, jt, 0:D + 1], start=False, stop=False)

                    if stop:
                        lo()
                        last = hi()
                    else:
                        hi()
                        last = lo()
                last.then_inc(pv_done, 1)

            def weigh_tile(b, w, k):
                jt = w * WT + k - UT
                if isinstance(jt, int):
                    jt %= NT
                weigh(b * NT + w * WT + k - UT, jt, k, start=isinstance(w, int) and w == 0 and k == UT,
                      stop=isinstance(w, int) and w == 0 and k == UT - 1)

            def step(b, w, ks=range(0, WT, 2), before=None):
                for k in ks:
                    masks(b, w, k)
                    scores(b, w, k)
                    scores(b, w, k + 1)
                    if before and k == UT:
                        before()
                    if not (first(b, w) and k < UT):
                        weigh_tile(b, w, k)
                        weigh_tile(b, w, k + 1)

            def rows_T(b):
                pe.wait_ge(x1_done, b + 1)
                wait_slot(slot_rows_T(b))
                for t in range(IT):
                    last = nc.tensor.transpose(S[0][:, t * P:(t + 1) * P], x1[:, t, :], ident[:, :])
                last.then_inc(slot_filled, 1)

            def sup(b):
                wait_slot(slot_sup(b))
                pe.wait_ge(slot_done, slot_rows_T(b) + 1)
                for t in range(IT):
                    last = nc.tensor.matmul(S[1][:, t * P:(t + 1) * P], x1T[:, t * P:(t + 1) * P], w_sb[:, :],
                                            start=True, stop=True)
                last.then_inc(slot_filled, 1)

            pe.wait_ge(pro, 17)
            pe.wait_ge(w_in, 16)
            step(0, 0)
            with pe.Fori(1, NW) as w:
                step(0, w)

            def outputs_free(b):
                pe.wait_ge(o_read_v, b)
                pe.wait_ge(o_read_a, b)

            with pe.Fori(1, NB) as b:
                step(b, 0, before=lambda: outputs_free(b))
                with pe.Fori(1, NW - 1) as w:
                    step(b, w)
                rows_T(b - 1)
                step(b, NW - 1, range(0, UT, 2))
                sup(b - 1)
                step(b, NW - 1, range(UT, WT, 2))
            for k in range(UT):
                weigh(NB * NT - UT + k, NT - UT + k, k, stop=k == UT - 1)

            def aggregate(r, m, slot):
                pe.wait_ge(adjb_v if m % 2 == 0 else adjb_a, r * (NR // 2) + m // 2 + 1)
                for j in range(2):
                    for t in range(IT):
                        last = nc.tensor.matmul(psum[:, CB[slot] + t // 2, (t % 2) * 256:(t % 2) * 256 + 256],
                                                adjb[m % NS][:, j, t * P:(t + 1) * P], sup_all[:, 2 * m + j, :],
                                                start=m == 0 and j == 0 and t % 2 == 0,
                                                stop=False, skip_group_check=True)
                last.then_inc(agg_done, 1)

            def round_(r, slot):
                if not isinstance(r, int) or r > 1:
                    pe.wait_ge(c_read, r - 1)
                for m in range(NR):
                    aggregate(r, m, slot)

            outputs_free(NB)
            for m in range(NR):
                if m == M_ROWS_T:
                    rows_T(NB - 1)
                if m == M_SUP:
                    sup(NB - 1)
                if 4 * m % NR == 0:
                    pe.wait_ge(sup_in[4 * m // NR], 16)
                if m == (NT - IT) // 2:
                    pe.wait_ge(sup_split, NB)
                aggregate(0, m, 0)
            round_(1, 1)
            with pe.Fori(1, NB // 2) as rr:
                round_(rr * 2, 0)
                round_(rr * 2 + 1, 1)


def kernel(x, adj, L0_gnn_beta, L1_gnn_weight):
    import numpy as np
    import concourse.bacc as bacc
    from concourse.bass_utils import run_bass_kernel_spmd

    nc = bacc.Bacc("TRN2", target_bir_lowering=False, num_devices=1)
    N, D = x.shape
    arrays = {"in_x": x, "in_adj": adj, "in_beta": L0_gnn_beta, "in_weight": L1_gnn_weight}
    arrays = {k: np.ascontiguousarray(v) for k, v in arrays.items()}
    aps = [nc.dram_tensor(k, v.shape, mybir.dt.from_np(v.dtype), kind="ExternalInput").ap() for k, v in arrays.items()]
    x1_dram = nc.dram_tensor("x1_rows", (N, D), F32).ap()
    sup_dram = nc.dram_tensor("support_parts", (N, 2 * D), F16).ap()
    q_dram = nc.dram_tensor("norms", (1, N), F32).ap()
    out = nc.dram_tensor("out", (N, D), F32, kind="ExternalOutput").ap()
    resnorm_graph_kernel(nc, *aps, x1_dram, sup_dram, q_dram, out)
    return run_bass_kernel_spmd(nc, [arrays], core_ids=[0]).results[0]["out"]
```

```python
from contextlib import ExitStack

import concourse.bass as bass
from concourse import mybir

F32 = mybir.dt.float32
F16 = mybir.dt.float16
BF16 = mybir.dt.bfloat16
U8 = mybir.dt.uint8
I32 = mybir.dt.int32
ALU = mybir.AluOpType
ACT = mybir.ActivationFunctionType
AX = mybir.AxisListType
RMAX = bass.bass_isa.ReduceOp.max
RADD = bass.bass_isa.ReduceOp.add

P = 128
EPS_LN = 1e-5
EPS_COS = 1e-7


def resnorm_graph_kernel(nc, x, adj, beta, weight, x1_dram, x1p_dram, q_dram, out):
    N, D = x.shape
    BI = 512
    NB = N // BI
    IT = BI // P
    NT = N // P
    UT = 4
    NU = NT // UT
    WT = 2 * UT
    NW = NT // WT
    XC = 2 * D + 1
    HB = BI // 2
    HT = IT // 2
    NC = 4
    CT = NT // NC
    ESC = 2.0 ** 15
    LSC = 2.0 ** 11
    USC = 2.0 ** 15
    assert CT == WT and D == P and NB % 2 == 0 and NW > 1

    with ExitStack() as ctx:
        def sb(name, shape, dt):
            return ctx.enter_context(nc.sbuf_tensor(name, shape, dt))

        def sem(name):
            return ctx.enter_context(nc.semaphore(name))

        adjT = sb("adjT", [P, NB, NT, BI], U8)
        stage = sb("stage", [P, 2, IT, UT * P], F32)
        uT = sb("uT", [P, 2, N], F16)
        xaug = sb("xaug", [P, NT, XC], F16)
        E = sb("E", [P, UT, BI], F32)
        eh = sb("eh", [P, UT, BI], F16)
        el = sb("el", [P, UT, BI], F16)
        xres = sb("xres", [P, IT, D], F32)
        h = sb("h", [P, IT, D], F32)
        x1 = sb("x1", [P, IT, D], F32)
        q_row = sb("q_row", [P, BI], F32)
        q_T = sb("q_T", [NT, P], F32)
        flag = sb("flag", [P, 1], I32)
        x1p = sb("x1p", [P, IT, 2, D], F16)
        w_sb = sb("w_sb", [P, D], F32)
        ident = sb("ident", [P, P], F32)
        identb = sb("identb", [P, P], BF16)
        n2 = sb("n2", [P, NT], F32)
        rn = sb("rn", [P, NT], F32)
        q = sb("q", [P, NT], F32)
        half_pow = sb("half_pow", [P, NT], F32)
        sc = sb("sc", [P, 11], F32)
        stats = sb("stats", [P, 8, 6], F32)
        mean = sb("mean", [P, 8], F32)
        tmp = sb("tmp", [P, 3, 8], F32)
        rstd = sb("rstd", [P, 8], F32)
        o_lo = sb("o_lo", [P, IT, D + 1], F32)
        sumT = o_lo[:, :, :].rearrange("p t d -> p (t d)")[:, 0:BI]
        shift = sb("shift", [P, IT], F32)
        rden = sb("rden", [P, IT], F32)

        xfull = adjT[:, NB - 1, :, :].rearrange("p t i -> p (t i)").bitcast(F32).rearrange("p (t d) -> p t d", d=D)
        work = adjT[:, NB - 2, :, :].rearrange("p t i -> p (t i)").bitcast(F32).rearrange("p (t d) -> p t d", d=D)
        x1p_all = uT[:, :, :].rearrange("p a (t d) -> p (a t) d", d=2 * D)
        x1p_last = x1p_all[:, NT - IT:NT, :].rearrange("p t (a d) -> p t a d", d=D)
        adjb = [part.rearrange("p a i -> p (a i)").bitcast(BF16).rearrange("p (s t i) -> p s t i", t=2, i=BI)[:, s]
                for part, n in ((E[:, :, :], UT), (eh[:, :, :], UT // 2), (el[:, :, :], UT // 2)) for s in range(n)]
        NS = len(adjb)
        NR = NT // 2
        M_W = 2

        C_RMAX, C_QMAX, C_G0, C_G1, C_PX, C_XS, C_XI, C_B, C_BS, C_BB, C_T2 = range(11)

        def col(c):
            return sc[:, c:c + 1]

        psum = ctx.enter_context(nc.psum_tensor("psum", [P, 8, 512], F32))
        S = [psum[:, b, :] for b in range(2)]
        T = [psum[:, 2 + b, :].bitcast(BF16).rearrange("p (t i) -> p t i", i=BI) for b in range(2)]
        O = [psum[:, 4 + b, :] for b in range(IT)]

        BT = [psum[:, 2 + s, :] for s in range(2)]
        C = [psum[:, 4 + s, :] for s in range(2)]
        BT_half = [BT[1], S[0]]
        C_half = [C[1], O[2]]

        x_in = [sem(f"x_in{c}") for c in range(NC)]
        w_in = sem("w_in")
        beta_in = sem("beta_in")
        adj_in = [sem(f"adj_in{b}") for b in range(2)]
        xres_in = sem("xres_in")
        consts = sem("consts")
        q_filled = sem("q_filled")
        q_moved = sem("q_moved")
        q_stored = sem("q_stored")
        q_row_in = sem("q_row_in")
        flag_set = sem("flag_set")
        half_scaled = sem("half_scaled")
        scaled = sem("scaled")
        fix = sem("fix")
        squares_v = sem("squares_v")
        squares_a = sem("squares_a")
        n2_done = sem("n2_done")
        rn_done = sem("rn_done")
        norms = sem("norms")
        maxima = sem("maxima")
        beta_ready = sem("beta_ready")
        xs_step = sem("xs_step")
        x_hi = sem("x_hi")
        x_lo = sem("x_lo")
        uT_filled = sem("uT_filled")
        uT_hi = sem("uT_hi")
        uT_lo = sem("uT_lo")
        slot_filled = sem("slot_filled")
        slot_done = sem("slot_done")
        mask_filled = sem("mask_filled")
        mask_stored = sem("mask_stored")
        masked = sem("masked")
        hi_v = sem("hi_v")
        hi_a = sem("hi_a")
        lo_done = sem("lo_done")
        pv_done = sem("pv_done")
        o_lo_read = sem("o_lo_read")
        o_read = sem("o_read")
        chain = sem("chain")
        stats_done = sem("stats_done")
        rstd_done = sem("rstd_done")
        shift_done = sem("shift_done")
        x1_done = sem("x1_done")
        x1_stored = sem("x1_stored")
        x1_hi = sem("x1_hi")
        x1_split = sem("x1_split")
        u_done = sem("u_done")
        x1p_stored = sem("x1p_stored")
        x1p_in = [sem(f"x1p_in{g}") for g in range(4)]
        adjb_v = sem("adjb_v")
        adjb_a = sem("adjb_a")
        agg_done = sem("agg_done")
        half_summed = sem("half_summed")
        last_rows = sem("last_rows")
        sum_moved = sem("sum_moved")
        c_done = sem("c_done")
        c_read = sem("c_read")
        x1_in = [sem(f"x1_in{b}") for b in range(2)]
        y_done = sem("y_done")
        y_half_stored = sem("y_half_stored")
        y_stored = [sem(f"y_stored{b}") for b in range(2)]

        adj_v = adj.rearrange("(b t p) (u c) -> b u p t c", p=P, t=IT, c=UT * P)
        x_v = x.rearrange("(b t p) d -> b p t d", p=P, t=IT)
        x1_v = x1_dram.rearrange("(b t p) d -> b p t d", p=P, t=IT)
        x1p_v = x1p_dram.rearrange("(b t p) d -> b p t d", p=P, t=IT)
        x1p_l = x1p_dram.rearrange("(t p) d -> p t d", p=P)
        q_v = q_dram.rearrange("a (t p) -> (a t) p", p=P)
        out_v = out.rearrange("(b t p) d -> b p t d", p=P, t=IT)

        block = ctx.enter_context(nc.Block())

        def last_block(b):
            return isinstance(b, int) and b == NB - 1

        def tile_of(b, w, k):
            return b * NT + w * WT + k

        PAIRS = [(w, k) for w in range(NW) for k in range(0, WT, 2)]

        def first(b, w):
            return isinstance(b, int) and b == 0 and isinstance(w, int) and w == 0

        def x1_parts(b):
            return x1p_last if last_block(b) else x1p

        U_BANK = [0, 1, 4, 5, 6, 7, 0, 1]
        LO_ORDER = [0, 1, 6, 7, 2, 3, 4, 5]
        assert len(U_BANK) == NT // 4

        def chunk(c):
            return slice(c * CT, (c + 1) * CT)

        @block.sync
        def _(sp):
            for c in range(NC):
                s = chunk(c)
                sp.dma_start(xfull[:, s, :], x.rearrange("(t p) d -> p t d", p=P)[:, s, :]).then_inc(x_in[c], 16)

            def load_unit(b, u, slot):
                sp.dma_start(stage[:, slot, :, :], adj_v[b, u, :, :, :]).then_inc(adj_in[slot], 16)

            def load_units(b, w):
                for s in range(2):
                    if not first(b, w):
                        sp.wait_ge(mask_filled, (b * NU + 2 * w + s - 1) * 2)
                    load_unit(b, 2 * w + s, s)

            def store_x1(b):
                sp.wait_ge(x1_done, b + 1)
                sp.dma_start(x1_v[b], x1[:, :, :]).then_inc(x1_stored, 16)

            def store_x1p(b):
                sp.wait_ge(x1_split, b + 1)
                sp.dma_start(x1p_v[b], x1p[:, :, :, :].rearrange("p t a d -> p t (a d)")).then_inc(x1p_stored, 16)

            def load_xres(b):
                sp.dma_start(xres[:, :, :], x_v[b]).then_inc(xres_in, 16)

            def load_q_row(b):
                if not isinstance(b, int) or b > 0:
                    sp.wait_ge(masked, NT * b)
                sp.dma_start(q_row[:, :], q_dram[0:1, bass.ds(b * BI, BI)].to_broadcast([P, BI])).then_inc(q_row_in, 16)

            load_xres(0)
            load_units(0, 0)
            sp.wait_ge(q_moved, 1)
            sp.dma_start(q_v, q_T[:, :]).then_inc(q_stored, 16)
            sp.wait_ge(q_stored, 16)
            load_q_row(0)
            with sp.Fori(1, NW) as w:
                load_units(0, w)
            def load_block(b):
                load_units(b, 0)
                load_q_row(b)
                if not isinstance(b, int) or b > 1:
                    store_x1(b - 2)
                    load_xres(b - 1)
                load_units(b, 1)
                if not isinstance(b, int) or b > 1:
                    store_x1p(b - 2)
                load_units(b, 2)
                load_units(b, 3)

            load_block(1)
            with sp.Fori(2, NB) as b:
                load_block(b)
            store_x1(NB - 2)
            load_xres(NB - 1)
            sp.wait_ge(slot_filled, NB * NT)
            sp.wait_ge(x1p_stored, 16 * (NB - 2))
            for g in range(3):
                s = slice(g * NT // 4, (g + 1) * NT // 4)
                sp.dma_start(x1p_all[:, s, :], x1p_l[:, s, :]).then_inc(x1p_in[g], 16)
            store_x1p(NB - 2)
            sp.wait_ge(x1p_stored, 16 * (NB - 1))
            s = slice(3 * NT // 4, NT - IT)
            sp.dma_start(x1p_all[:, s, :], x1p_l[:, s, :]).then_inc(x1p_in[3], 16)
            store_x1(NB - 1)
            sp.wait_ge(x1_stored, 16 * NB)

            def load_x1(r, slot):
                sp.dma_start(stage[:, slot, :, 0:D], x1_v[r]).then_inc(x1_in[slot], 16)

            def store_y(r, slot):
                sp.wait_ge(y_done, r + 1)
                sp.dma_start(out_v[r], stage[:, slot, :, 2 * D:3 * D]).then_inc(y_stored[slot], 16)

            load_x1(0, 0)
            load_x1(1, 1)
            with sp.Fori(1, NB // 2) as rr:
                for s in range(2):
                    store_y(rr * 2 + s - 2, s)
                    sp.wait_ge(y_stored[s], rr * 16)
                    load_x1(rr * 2 + s, s)
            store_y(NB - 2, 0)
            for half in range(2):
                t = slice(half * HT, (half + 1) * HT)
                sp.wait_ge(y_done, NB + half)
                sp.dma_start(out_v[NB - 1][:, t, :], stage[:, 1, t, 2 * D:3 * D]).then_inc(y_half_stored, 16)
            sp.wait_ge(y_stored[0], 8 * NB)
            sp.wait_ge(y_stored[1], 8 * NB - 16)
            sp.wait_ge(y_half_stored, 32)

        @block.gpsimd
        def _(pool):
            nc.gpsimd.memset(ident[:, :], 0.0).then_inc(consts, 1)
            nc.gpsimd.memset(xaug[:, :, D:D + 1], 1.0).then_inc(consts, 1)
            nc.gpsimd.memset(half_pow[:, :], -0.5).then_inc(consts, 1)
            pool.wait_ge(consts, 3)
            nc.gpsimd.affine_select(out=ident[:, :], in_=ident[:, :], compare_op=ALU.not_equal, fill=1.0,
                                    base=0, pattern=[[-1, P]], channel_multiplier=1).then_inc(consts, 1)
            pool.wait_ge(consts, 4)
            nc.gpsimd.tensor_copy(identb[:, :], ident[:, :]).then_inc(consts, 1)
            for c in range(NC):
                pool.wait_ge(n2_done, c + 1)
                nc.gpsimd.tensor_tensor(rn[:, chunk(c)], n2[:, chunk(c)], half_pow[:, chunk(c)],
                                        ALU.pow).then_inc(rn_done, 1)
            pool.wait_ge(norms, 3)
            nc.gpsimd.partition_all_reduce(sc[:, C_G0:C_G0 + 2], sc[:, C_RMAX:C_RMAX + 2], P, RMAX).then_inc(maxima, 1)
            def power(done, o, n):
                pool.wait_ge(stats_done, done)
                nc.gpsimd.tensor_tensor(rstd[:, o:o + n], rstd[:, o:o + n], half_pow[:, 0:n], ALU.pow).then_inc(rstd_done, 1)

            def rows(b):
                power(b + 1, 0, IT)
                dst = x1_parts(b)
                pool.wait_ge(x1_hi, b + 1)
                nc.gpsimd.tensor_tensor(dst[:, :, 1, :], x1[:, :, :], dst[:, :, 0, :], ALU.subtract).then_inc(x1_split, 1)

            with pool.Fori(0, NB - 1) as b:
                rows(b)
            power(NB, 0, IT)
            for r in range(NB - 1):
                power(NB + r + 1, IT * (r % 2), IT)
            for half in range(2):
                power(2 * NB + half, IT + half * HT, HT)

        @block.scalar
        def _(act):
            act.dma_start(col(C_B), beta.rearrange("(a b) -> a b", a=1).to_broadcast([P, 1])).then_inc(beta_in, 16)
            act.dma_start(w_sb[:, :], weight).then_inc(w_in, 16)
            for c, tiles in ((NC - 2, chunk(NC - 2)), (NC - 1, slice(NT - CT // 2, NT))):
                act.wait_ge(x_in[c], 16)
                for t in range(tiles.start, tiles.stop):
                    last = nc.scalar.activation(work[:, t, :], xfull[:, t, :], ACT.Square, accum_out=n2[:, t:t + 1])
                last.then_inc(squares_a, 1)
            for g in range(NT // 4):
                if g == 6:
                    act.wait_ge(q_filled, 1)
                    nc.scalar.activation(q_T[:, :], psum[0:NT, 3, 0:P], ACT.Copy).then_inc(q_moved, 1)
                act.wait_ge(uT_filled, g + 1)
                nc.scalar.activation(uT[:, 0, g * 512:(g + 1) * 512], psum[:, U_BANK[g], :], ACT.Copy).then_inc(uT_hi, 1)

            act.wait_ge(beta_ready, 2)
            act.wait_ge(flag_set, 1)
            small = act.value_load(flag[0:1, 0:1], min_val=0, max_val=1)

            def exp_tile(b, w, k):
                c = tile_of(b, w, k)
                n = b * NT + w * WT + k
                act.wait_ge(slot_filled, c + 1)
                act.wait_ge(scaled, (n + 1) * small + 1)
                if not (first(b, w) and k < UT):
                    act.wait_ge(lo_done, n - UT + 1)
                nc.scalar.activation(E[:, k % UT, :], S[k % 2], ACT.Exp,
                                     bias=col(C_BB), scale=col(C_BS)).then_inc(slot_done, 1)

            def store_masks(b, w, k):
                p = (b * NT + w * WT + k) // 2 if isinstance(b, int) and isinstance(w, int) else b * (NT // 2) + w * UT + k // 2
                act.wait_ge(mask_filled, p + 1)
                nc.scalar.activation(adjT[:, b, bass.ds(w * WT + k, 2), :], T[(k // 2) % 2], ACT.Copy).then_inc(mask_stored, 1)

            def split_x1_hi(b):
                act.wait_ge(x1_done, b + 1)
                if not isinstance(b, int) or b > 0:
                    act.wait_ge(x1p_stored, 16 * b)
                nc.scalar.activation(x1_parts(b)[:, :, 0, :], x1[:, :, :], ACT.Copy).then_inc(x1_hi, 1)

            def read_out(b):
                act.wait_ge(pv_done, (b + 1) * NT)
                if not isinstance(b, int) or b > 0:
                    act.wait_ge(o_read, b)
                for half in range(2):
                    nc.scalar.activation(o_lo[:, half * HT:(half + 1) * HT, :],
                                         psum[:, 4 + half * HT:4 + (half + 1) * HT, D:XC],
                                         ACT.Copy).then_inc(o_lo_read, 1)

            def normalise(b, ts):
                if 0 in ts:
                    act.wait_ge(shift_done, b + 1)
                    if not isinstance(b, int) or b > 0:
                        act.wait_ge(x1_stored, 16 * b)
                        act.wait_ge(x1_split, b)
                for t in ts:
                    last = nc.scalar.activation(x1[:, t, :], h[:, t, :], ACT.Identity, bias=shift[:, t:t + 1],
                                                scale=rstd[:, t:t + 1])
                if IT - 1 in ts:
                    last.then_inc(x1_done, 1)

            def split_hi(b, w, k):
                n = b * NT + w * WT + k
                act.wait_ge(masked, n + 1)
                if not (first(b, w) and k < UT):
                    act.wait_ge(pv_done, n - UT + 1)
                nc.scalar.activation(eh[:, k % UT, :], E[:, k % UT, :], ACT.Copy).then_inc(hi_a, 1)

            def pair(b, w, k):
                store_masks(b, w, k)
                exp_tile(b, w, k)
                if not (first(b, w) and k == 0):
                    split_hi(b, w, k - 1)
                exp_tile(b, w, k + 1)

            def xaug_hi(c):
                part = bass.ds(c * CT, CT)
                act.wait_ge(xs_step, 3)
                nc.scalar.activation(xaug[:, part, 0:D], xfull[:, part, :], ACT.Copy, scale=col(C_XS)).then_inc(x_hi, 1)

            def step(w, chunks={}):
                for k in range(0, WT, 2):
                    pair(0, w, k)
                    if k in chunks:
                        xaug_hi(chunks[k])

            step(0, {0: 0, UT + 2: 1})
            with act.Fori(1, NW - 1) as w:
                step(w, {UT + 2: w + 1})
            step(NW - 1)
            with act.Fori(1, NB) as b:
                for w, k in PAIRS:
                    pair(b, w, k)
                    if (w, k) == PAIRS[1]:
                        read_out(b - 1)
                    for t in range(IT):
                        if (w, k) == PAIRS[10 + t]:
                            normalise(b - 1, [t])
                    if (w, k) == PAIRS[15]:
                        split_x1_hi(b - 1)
            split_hi(NB - 1, NW, -1)

            def widen(r, m):
                if not (isinstance(r, int) and r == 0 and m < NS):
                    act.wait_ge(agg_done, r * NR + m - NS + 1)
                nc.scalar.activation(adjb[m % NS], adjT[:, r, 2 * m:2 * m + 2, :], ACT.Copy).then_inc(adjb_a, 1)

            act.wait_ge(lo_done, NB * NT - 2)
            widen(0, 1)
            act.wait_ge(lo_done, NB * NT)
            widen(0, 3)
            read_out(NB - 1)
            for m in range(5, NR, 2):
                widen(0, m)
                if m == NS + 1:
                    normalise(NB - 1, range(IT))
                if m == NR - 3:
                    split_x1_hi(NB - 1)

            def move_sum(r, slot):
                act.wait_ge(agg_done, (r + 1) * NR)
                if not isinstance(r, int) or r > 0:
                    act.wait_ge(c_done, r)
                nc.scalar.activation(sumT[:, :], BT[slot], ACT.Copy).then_inc(sum_moved, 1)

            def round_(r, slot):
                for m in range(1, NR, 2):
                    if m == NS - 1:
                        move_sum(r - 1, 1 - slot)
                    widen(r, m)

            round_(1, 1)
            round_(2, 0)
            with act.Fori(1, NB // 2 - 1) as rr:
                round_(rr * 2 + 1, 1)
                round_(rr * 2 + 2, 0)
            round_(NB - 1, 1)
            for half in range(2):
                act.wait_ge(half_summed, half + 1)
                act.wait_ge(c_done, NB - 1)
                nc.scalar.activation(sumT[:, half * HB:(half + 1) * HB], BT_half[half][:, 0:HB],
                                     ACT.Copy).then_inc(sum_moved, 1)

        @block.vector
        def _(dve):
            dve.wait_ge(beta_in, 16)
            nc.vector.tensor_scalar_mul(col(C_BS), col(C_B), 1.0 / (USC * USC)).then_inc(beta_ready, 1)
            nc.vector.tensor_scalar(col(C_BB), col(C_B), -1.0, col(C_B), ALU.mult, ALU.min).then_inc(beta_ready, 1)

            def sum_squares(c, n=CT):
                dve.wait_ge(x_in[c], 16)
                for t in range(c * CT, c * CT + n):
                    last = nc.vector.tensor_tensor_reduce(out=work[:, t, :], in0=xfull[:, t, :], in1=xfull[:, t, :],
                                                          scale=1.0, scalar=0.0, op0=ALU.mult, op1=ALU.add,
                                                          accum_out=n2[:, t:t + 1])
                last.then_inc(squares_v, 1)

            def clamp(c, by_v, by_a):
                if by_v:
                    dve.wait_ge(squares_v, by_v)
                if by_a:
                    dve.wait_ge(squares_a, by_a)
                nc.vector.tensor_scalar_max(n2[:, chunk(c)], n2[:, chunk(c)], 1e-36).then_inc(n2_done, 1)

            def unit_rows(c):
                dve.wait_ge(rn_done, c + 1)
                nc.vector.scalar_tensor_tensor(out=work[:, chunk(c), :], in0=xfull[:, chunk(c), :], scalar=USC,
                                               in1=rn[:, chunk(c)].unsqueeze(2).to_broadcast([P, CT, D]),
                                               op0=ALU.mult, op1=ALU.mult).then_inc(u_done, 1)

            def uT_lo_part(n):
                g = LO_ORDER[n]
                dve.wait_ge(uT_hi, g + 1)
                nc.vector.tensor_tensor(uT[:, 1, g * 512:(g + 1) * 512], psum[:, U_BANK[g], :],
                                        uT[:, 0, g * 512:(g + 1) * 512], ALU.subtract).then_inc(uT_lo, 1)

            sum_squares(0)
            clamp(0, 1, 0)
            sum_squares(1)
            clamp(1, 2, 0)
            unit_rows(0)
            sum_squares(NC - 1, CT // 2)
            clamp(2, 0, 1)
            unit_rows(1)
            clamp(3, 3, 2)
            uT_lo_part(0)
            unit_rows(2)
            dve.wait_ge(rn_done, NC)
            nc.vector.reciprocal(q[:, :], rn[:, :]).then_inc(norms, 1)
            nc.vector.reduce_max(col(C_RMAX), rn[:, :], AX.X).then_inc(norms, 1)
            dve.wait_ge(norms, 1)
            nc.vector.reduce_max(col(C_QMAX), q[:, :], AX.X).then_inc(norms, 1)
            unit_rows(3)
            uT_lo_part(1)
            dve.wait_ge(maxima, 1)
            nc.vector.tensor_scalar(sc[:, C_PX:C_PX + 1].bitcast(I32), col(C_G1).bitcast(I32), 0x7F800000, None,
                                    ALU.bitwise_and).then_inc(xs_step, 1)
            nc.vector.tensor_tensor(col(C_T2), col(C_G0), col(C_G0), ALU.mult).then_inc(fix, 1)
            dve.wait_ge(xs_step, 1)
            nc.vector.tensor_scalar_mul(col(C_XI), col(C_PX), 2.0 ** -14).then_inc(xs_step, 1)
            dve.wait_ge(fix, 1)
            nc.vector.tensor_scalar(flag[:, :], col(C_T2), 0.5, None, ALU.is_gt).then_inc(flag_set, 1)
            dve.wait_ge(xs_step, 2)
            nc.vector.reciprocal(col(C_XS), col(C_XI)).then_inc(xs_step, 1)
            dve.wait_ge(flag_set, 1)
            nc.vector.tensor_copy(col(C_T2), flag[:, :]).then_inc(scaled, 1)
            uT_lo_part(2)
            uT_lo_part(3)
            small = dve.value_load(flag[0:1, 0:1], min_val=0, max_val=1)
            for n in range(4, NT // 4):
                uT_lo_part(n)


            def add_small_term(b, w, k):
                n = b * NT + w * WT + k
                dve.wait_ge(slot_filled, tile_of(b, w, k) + 1)
                dve.wait_ge(q_row_in, 16 * (b + 1))
                if not (first(b, w) and k < UT):
                    dve.wait_ge(lo_done, n - UT + 1)
                num, den = E[:, k % UT, 0:HB], E[:, k % UT, HB:BI]
                s = S[k % 2]
                for half in range(2):
                    base = 1 + 8 * n + 4 * half
                    part = slice(half * HB, (half + 1) * HB)
                    nc.vector.tensor_scalar_mul(num, q_row[:, part], q[:, bass.ds(w * WT + k, 1)]).then_inc(fix, 1)
                    dve.wait_ge(fix, base + 1)
                    nc.vector.tensor_scalar_add(den, num, EPS_COS).then_inc(fix, 1)
                    dve.wait_ge(fix, base + 2)
                    nc.vector.reciprocal(den, den).then_inc(fix, 1)
                    dve.wait_ge(fix, base + 3)
                    nc.vector.tensor_tensor(num, num, den, ALU.mult).then_inc(fix, 1)
                    dve.wait_ge(fix, base + 4)
                    done = nc.vector.tensor_tensor(s[:, part], s[:, part], num, ALU.mult)
                    done.then_inc(half_scaled, 1) if half == 0 else done.then_inc(scaled, 1)
                    if half == 0:
                        dve.wait_ge(half_scaled, n + 1)

            def mask_tile(b, w, k):
                n = b * NT + w * WT + k
                with dve.If(small > 0):
                    add_small_term(b, w, k)
                p = b * (NT // 2) + w * UT + k // 2
                dve.wait_ge(slot_done, tile_of(b, w, k) + 1)
                dve.wait_ge(mask_stored, p + 1)
                nc.vector.scalar_tensor_tensor(out=E[:, k % UT, :], in0=E[:, k % UT, :], scalar=ESC,
                                               in1=adjT[:, b, w * WT + k, :], op0=ALU.mult,
                                               op1=ALU.mult).then_inc(masked, 1)

            def split_hi(b, w, k):
                n = b * NT + w * WT + k
                dve.wait_ge(masked, n + 1)
                if not (first(b, w) and k < UT):
                    dve.wait_ge(pv_done, n - UT + 1)
                nc.vector.tensor_copy(eh[:, k % UT, :], E[:, k % UT, :]).then_inc(hi_v, 1)

            def split_lo(b, w, k):
                half = b * (NT // 2) + w * (WT // 2)
                dve.wait_ge(hi_v if k % 2 == 0 else hi_a, half + (k // 2 + 1 if k > 0 else 1 if k == 0 else 0))
                nc.vector.tensor_tensor(el[:, k % UT, :], E[:, k % UT, :], eh[:, k % UT, :],
                                        ALU.subtract).then_inc(lo_done, 1)

            def pair(b, w, k, amid=None):
                mask_tile(b, w, k)
                if not (first(b, w) and k == 0):
                    split_lo(b, w, k - 1)
                if amid:
                    amid()
                split_hi(b, w, k)
                mask_tile(b, w, k + 1)
                split_lo(b, w, k)

            def moments(src, o, ts, base):
                for t in ts:
                    last = nc.vector.bn_stats(stats[:, o + t, :], src(t))
                if IT - 1 in ts:
                    last.then_inc(chain, 1)

            def combine(o, base, n=IT, order=chain):
                dve.wait_ge(order, base + 1)
                s_ = slice(o, o + n)
                nc.vector.tensor_tensor(tmp[:, 0, s_], stats[:, s_, 1], stats[:, s_, 4], ALU.add)
                nc.vector.tensor_tensor(tmp[:, 1, s_], stats[:, s_, 1], stats[:, s_, 4], ALU.subtract)
                nc.vector.tensor_tensor(tmp[:, 2, s_], stats[:, s_, 2], stats[:, s_, 5], ALU.add).then_inc(order, 1)

            def scale_eps(scale):
                return EPS_LN * scale if scale < 1.0 else EPS_LN * LSC * LSC

            def mean_var(o, base, n=IT, order=chain, scale=1.0):
                s_ = slice(o, o + n)
                dve.wait_ge(order, base + 2)
                nc.vector.tensor_scalar(tmp[:, 2, s_], tmp[:, 2, s_], scale / D, scale_eps(scale), ALU.mult, ALU.add)
                nc.vector.scalar_tensor_tensor(out=tmp[:, 1, s_], in0=tmp[:, 1, s_], scalar=0.25 * scale,
                                               in1=tmp[:, 1, s_], op0=ALU.mult, op1=ALU.mult)
                nc.vector.tensor_scalar_mul(mean[:, s_], tmp[:, 0, s_], 0.5).then_inc(order, 1)

            def variance(o, base, n=IT, order=chain):
                s_ = slice(o, o + n)
                dve.wait_ge(order, base + 3)
                nc.vector.tensor_tensor(rstd[:, s_], tmp[:, 1, s_], tmp[:, 2, s_], ALU.add).then_inc(stats_done, 1)

            def read_out(b):
                if not isinstance(b, int) or b > 0:
                    dve.wait_ge(x1_done, b)
                for half in range(2):
                    t = slice(half * HT, (half + 1) * HT)
                    dve.wait_ge(o_lo_read, 2 * b + half + 1)
                    last = nc.vector.tensor_tensor(h[:, t, :], psum[:, 4 + half * HT:4 + (half + 1) * HT, 0:D],
                                                   o_lo[:, t, 1:D + 1], ALU.add)
                last.then_inc(o_read, 1)
                nc.vector.reciprocal(rden[:, :], o_lo[:, :, 0]).then_inc(chain, 1)

            def scale_den(b):
                dve.wait_ge(chain, 6 * b + 1)
                nc.vector.tensor_scalar_mul(rden[:, :], rden[:, :], col(C_XI)).then_inc(chain, 1)

            def residual(b, ts):
                dve.wait_ge(o_read, b + 1)
                dve.wait_ge(chain, 6 * b + 2)
                dve.wait_ge(xres_in, 16 * (b + 1))
                for t in ts:
                    last = nc.vector.scalar_tensor_tensor(out=h[:, t, :], in0=h[:, t, :], scalar=rden[:, t:t + 1],
                                                          in1=xres[:, t, :], op0=ALU.mult, op1=ALU.add)
                if IT - 1 in ts:
                    last.then_inc(chain, 1)

            def row_moments(b, ts):
                dve.wait_ge(chain, 6 * b + 3)
                moments(lambda t: h[:, t, :], 0, ts, 6 * b + 3)

            def row_shift(b):
                dve.wait_ge(rstd_done, b + 1)
                nc.vector.scalar_tensor_tensor(out=shift[:, :], in0=mean[:, 0:IT], scalar=-1.0, in1=rstd[:, 0:IT],
                                               op0=ALU.mult, op1=ALU.mult).then_inc(shift_done, 1)

            def pieces(b):
                return [lambda: scale_den(b),
                        lambda: residual(b, range(0, IT // 2)), lambda: residual(b, range(IT // 2, IT)),
                        lambda: row_moments(b, range(0, IT // 2)), lambda: row_moments(b, range(IT // 2, IT)),
                        lambda: combine(0, 6 * b + 3), lambda: mean_var(0, 6 * b + 3, scale=1.0 / (LSC * LSC)),
                        lambda: variance(0, 6 * b + 3), lambda: row_shift(b)]

            def xaug_lo(c):
                part = bass.ds(c * CT, CT)
                dve.wait_ge(x_hi, c + 1)
                nc.vector.scalar_tensor_tensor(out=xaug[:, part, D + 1:XC], in0=xfull[:, part, :],
                                               scalar=col(C_XS), in1=xaug[:, part, 0:D], op0=ALU.mult,
                                               op1=ALU.subtract).then_inc(x_lo, 1)

            def step(w, chunks={}):
                for k in range(0, WT, 2):
                    pair(0, w, k)
                    if k in chunks:
                        xaug_lo(chunks[k])

            step(0, {0: 0, UT + 2: 1})
            with dve.Fori(1, NW - 1) as w:
                step(w, {UT + 2: w + 1})
            step(NW - 1)
            with dve.Fori(1, NB) as b:
                piece = pieces(b - 1)
                amid = {PAIRS[1]: lambda: read_out(b - 1), PAIRS[2]: piece[0], PAIRS[7]: piece[5], PAIRS[8]: piece[7],
                        PAIRS[9]: piece[8]}
                after = {PAIRS[3]: piece[1], PAIRS[4]: piece[2], PAIRS[5]: piece[3], PAIRS[6]: piece[4],
                         PAIRS[7]: piece[6]}
                for w, k in PAIRS:
                    pair(b, w, k, amid=amid.get((w, k)))
                    if (w, k) in after:
                        after[w, k]()
            split_lo(NB - 1, NW, -1)

            def widen(r, m):
                if not (isinstance(r, int) and r == 0 and m < NS):
                    dve.wait_ge(agg_done, r * NR + m - NS + 1)
                elif m == 0:
                    dve.wait_ge(lo_done, NB * NT - 3)
                elif m == 2:
                    dve.wait_ge(lo_done, NB * NT - 1)
                elif m == UT:
                    dve.wait_ge(pv_done, NB * NT)
                nc.vector.tensor_copy(adjb[m % NS], adjT[:, r, 2 * m:2 * m + 2, :]).then_inc(adjb_v, 1)

            def normalise_rows(slot, ts):
                st = stage[:, slot, :, :]
                for t in ts:
                    o = IT * slot + t
                    last = nc.vector.tensor_scalar(st[:, t, 2 * D:3 * D], st[:, t, D:2 * D], mean[:, o:o + 1],
                                                   rstd[:, o:o + 1], ALU.subtract, ALU.mult)
                last.then_inc(y_done, 1)

            def y_pieces(r, slot):
                base = 6 * NB + 3 * r
                st = stage[:, slot, :, :]

                def add():
                    dve.wait_ge(c_done, r + 1)
                    dve.wait_ge(x1_in[slot], 16 * (r // 2 + 1) if isinstance(r, int) else 8 * (r - slot) + 16)
                    nc.vector.tensor_tensor(st[:, :, D:2 * D], C[slot].rearrange("p (t d) -> p t d", d=D),
                                            st[:, :, 0:D], ALU.add).then_inc(c_read, 1)

                def row_moments():
                    dve.wait_ge(c_read, r + 1)
                    moments(lambda t: st[:, t, D:2 * D], IT * slot, range(IT), base)

                def mean_variance():
                    combine(IT * slot, base)
                    mean_var(IT * slot, base)
                    variance(IT * slot, base)

                def normalise():
                    dve.wait_ge(rstd_done, NB + r + 1)
                    normalise_rows(slot, range(IT))

                return add, lambda: (row_moments(), mean_variance()), normalise

            widen(0, 0)
            widen(0, 2)
            widen(0, 4)
            read_out(NB - 1)
            piece = pieces(NB - 1)
            for m in range(2, NR, 2):
                if m > 4:
                    widen(0, m)
                if m == NR - 2:
                    dve.wait_ge(x1_hi, NB)
                    nc.vector.tensor_tensor(x1p_last[:, :, 1, :], x1[:, :, :], x1p_last[:, :, 0, :],
                                            ALU.subtract).then_inc(x1_split, 1)
                for part in {2: piece[0:3], 4: piece[3:5], 6: piece[5:8], NS: piece[8:9]}.get(m, []):
                    part()

            def round_(r, slot):
                after = dict(zip((NS + M_W, NS + M_W + 2, NS + M_W + 4), y_pieces(r - 1, 1 - slot)))
                for m in range(0, NR, 2):
                    widen(r, m)
                    if m in after:
                        after[m]()

            with dve.Fori(0, NB // 2 - 1) as rr:
                round_(rr * 2 + 1, 1)
                round_(rr * 2 + 2, 0)
            round_(NB - 1, 1)
            st = stage[:, 1, :, :]
            dve.wait_ge(x1_in[1], 8 * NB)
            for half in range(2):
                ts = range(half * HT, (half + 1) * HT)
                base = 4 * half
                t_ = slice(half * HT, (half + 1) * HT)
                dve.wait_ge(c_done, NB + half)
                nc.vector.tensor_tensor(st[:, t_, D:2 * D], C_half[half][:, 0:HB].rearrange("p (t d) -> p t d", d=D),
                                        st[:, t_, 0:D], ALU.add).then_inc(last_rows, 1)
                dve.wait_ge(last_rows, base + 1)
                for t in ts:
                    last = nc.vector.bn_stats(stats[:, IT + t, :], st[:, t, D:2 * D])
                last.then_inc(last_rows, 1)
                combine(IT + half * HT, base + 1, HT, last_rows)
                mean_var(IT + half * HT, base + 1, HT, last_rows)
                variance(IT + half * HT, base + 1, HT, last_rows)
                dve.wait_ge(rstd_done, 2 * NB + half)
                normalise_rows(1, ts)

        @block.tensor
        def _(pe):
            pe.wait_ge(consts, 4)
            for g in range(NT // 4):
                if g == 6:
                    pe.wait_ge(norms, 1)
                    nc.tensor.transpose(psum[0:NT, 3, 0:P], q[:, :], ident[:, :]).then_inc(q_filled, 1)
                pe.wait_ge(u_done, g * 4 // CT + 1)
                if g >= 6:
                    pe.wait_ge(uT_lo, g - 5)
                for t in range(4):
                    last = nc.tensor.transpose(psum[:, U_BANK[g], t * P:(t + 1) * P], work[:, 4 * g + t, :], ident[:, :])
                last.then_inc(uT_filled, 1)
            pe.wait_ge(consts, 5)

            def masks(b, w, k):
                p = b * (NT // 2) + w * UT + k // 2
                s = k // UT
                if not (first(b, w) and k < 4):
                    pe.wait_ge(mask_stored, p - 1)
                if k % UT == 0:
                    pe.wait_ge(adj_in[s], (b * NW + w + 1) * 16)
                for kk in (k, k + 1):
                    for t in range(IT):
                        c = kk % UT
                        src = stage[:, s, t, c * P:(c + 1) * P].bitcast(BF16)[:, 1::2]
                        last = nc.tensor.transpose(T[(k // 2) % 2][:, kk % 2, t * P:(t + 1) * P], src, identb[:, :])
                last.then_inc(mask_filled, 1)

            def wait_slot(c):
                if not isinstance(c, int) or c >= 2:
                    pe.wait_ge(slot_done, c - 1)

            def scores(b, w, k):
                c = tile_of(b, w, k)
                wait_slot(c)
                j = (w * WT + k) * P
                i = b * BI
                o = S[k % 2]
                hj, lj = uT[:, 0, bass.ds(j, P)], uT[:, 1, bass.ds(j, P)]
                hi, li = uT[:, 0, bass.ds(i, BI)], uT[:, 1, bass.ds(i, BI)]
                nc.tensor.matmul(o, hj, hi, start=True, stop=False)
                nc.tensor.matmul(o, hj, li, start=False, stop=False)
                nc.tensor.matmul(o, lj, hi, start=False, stop=True).then_inc(slot_filled, 1)

            def weigh(n, jt, k, start=False, stop=False):
                pe.wait_ge(lo_done, n + 1)
                for t in range(IT):
                    def hi():
                        return nc.tensor.matmul(O[t][:, 0:XC], eh[:, k % UT, t * P:(t + 1) * P], xaug[:, jt, :],
                                                start=start, stop=stop)

                    def lo():
                        return nc.tensor.matmul(O[t][:, 0:D + 1], el[:, k % UT, t * P:(t + 1) * P],
                                                xaug[:, jt, 0:D + 1], start=False, stop=False)

                    if stop:
                        lo()
                        last = hi()
                    else:
                        hi()
                        last = lo()
                last.then_inc(pv_done, 1)

            def weigh_tile(b, w, k):
                jt = w * WT + k - UT
                if isinstance(jt, int):
                    jt %= NT
                weigh(b * NT + w * WT + k - UT, jt, k, start=isinstance(w, int) and w == 0 and k == UT,
                      stop=isinstance(w, int) and w == 0 and k == UT - 1)

            def pair(b, w, k, before=None):
                if first(b, w) and k == 2:
                    pe.wait_ge(q_moved, 1)
                masks(b, w, k)
                if first(b, w) and k == 0:
                    pe.wait_ge(uT_lo, 3)
                scores(b, w, k)
                if first(b, w) and k == 0:
                    pe.wait_ge(uT_lo, 4)
                scores(b, w, k + 1)
                if before:
                    before()
                if not (first(b, w) and k < UT):
                    weigh_tile(b, w, k)
                    weigh_tile(b, w, k + 1)

            def outputs_usable():
                pe.wait_ge(uT_lo, NT // 4)
                pe.wait_ge(x_lo, 1)

            for k in range(0, WT, 2):
                pair(0, 0, k, before=outputs_usable if k == UT else None)
            pe.wait_ge(w_in, 16)
            with pe.Fori(1, NW) as w:
                for k in range(0, WT, 2):
                    pair(0, w, k, before=(lambda: pe.wait_ge(x_lo, w + 1)) if k == UT else None)

            def outputs_free(b):
                pe.wait_ge(o_read, b)

            with pe.Fori(1, NB) as b:
                for w, k in PAIRS:
                    pair(b, w, k, before=(lambda: outputs_free(b)) if (w, k) == (0, UT) else None)
            for k in range(UT):
                weigh(NB * NT - UT + k, NT - UT + k, k, stop=k == UT - 1)

            def aggregate(r, m, out, half=None):
                pe.wait_ge(adjb_v if m % 2 == 0 else adjb_a, r * (NR // 2) + m // 2 + 1)
                cols = slice(0, BI) if half is None else slice(half * HB, (half + 1) * HB)
                for j in range(2):
                    for part in range(2):
                        last = nc.tensor.matmul(out, x1p_all[:, 2 * m + j, part * D:(part + 1) * D],
                                                adjb[m % NS][:, j, cols], start=m == 0 and j == 0 and part == 0,
                                                stop=m == NR - 1 and j == 1 and part == 1)
                return last

            def weights(r, out, ts=range(IT), n=None):
                pe.wait_ge(sum_moved, n or r + 1)
                if not isinstance(r, int) or r > 1:
                    pe.wait_ge(c_read, r - 1)
                for k, t in enumerate(ts):
                    last = nc.tensor.matmul(out[:, k * P:(k + 1) * P], sumT[:, t * P:(t + 1) * P], w_sb[:, :],
                                            start=True, stop=True)
                last.then_inc(c_done, 1)

            def round_(r, slot):
                for m in range(NR):
                    if m == M_W:
                        weights(r - 1, C[1 - slot])
                    aggregate(r, m, BT[slot]).then_inc(agg_done, 1)

            pe.wait_ge(mask_stored, NB * NT // 2)
            for m in range(NR):
                if 4 * m % NR == 0:
                    pe.wait_ge(x1p_in[4 * m // NR], 16)
                if m == (NT - IT) // 2:
                    pe.wait_ge(x1_split, NB)
                aggregate(0, m, BT[0]).then_inc(agg_done, 1)
            outputs_free(NB)
            round_(1, 1)
            round_(2, 0)
            with pe.Fori(1, NB // 2 - 1) as rr:
                round_(rr * 2 + 1, 1)
                round_(rr * 2 + 2, 0)
            for m in range(NR - NS):
                if m == M_W:
                    weights(NB - 2, C[0])
                aggregate(NB - 1, m, BT_half[0][:, 0:HB], 0)
                aggregate(NB - 1, m, BT_half[1][:, 0:HB], 1).then_inc(agg_done, 1)
            for half in range(2):
                for m in range(NR - NS, NR):
                    if half == 1 and m == NR - NS + 3:
                        weights(NB - 1, C_half[0], range(0, HT), NB)
                    last = aggregate(NB - 1, m, BT_half[half][:, 0:HB], half)
                last.then_inc(half_summed, 1)
            weights(NB - 1, C_half[1], range(HT, IT), NB + 1)


def kernel(x, adj, L0_gnn_beta, L1_gnn_weight):
    import numpy as np
    import concourse.bacc as bacc
    from concourse.bass_utils import run_bass_kernel_spmd

    nc = bacc.Bacc("TRN2", target_bir_lowering=False, num_devices=1)
    N, D = x.shape
    arrays = {"in_x": x, "in_adj": adj, "in_beta": L0_gnn_beta, "in_weight": L1_gnn_weight}
    arrays = {k: np.ascontiguousarray(v) for k, v in arrays.items()}
    aps = [nc.dram_tensor(k, v.shape, mybir.dt.from_np(v.dtype), kind="ExternalInput").ap() for k, v in arrays.items()]
    x1_dram = nc.dram_tensor("x1_rows", (N, D), F32).ap()
    x1p_dram = nc.dram_tensor("x1_parts", (N, 2 * D), F16).ap()
    q_dram = nc.dram_tensor("norms", (1, N), F32).ap()
    out = nc.dram_tensor("out", (N, D), F32, kind="ExternalOutput").ap()
    resnorm_graph_kernel(nc, *aps, x1_dram, x1p_dram, q_dram, out)
    return run_bass_kernel_spmd(nc, [arrays], core_ids=[0]).results[0]["out"]
```
